# Optimizing a Trainium2 kernel written in Bass

```python
import numpy as np
import jax
import jax.numpy as jnp

def _softmax(x, axis=-1):
    return jax.nn.softmax(x, axis=axis)

def _gelu(x):
    return jax.nn.gelu(x, approximate=True)

def _silu(x):
    return jax.nn.silu(x)

def _sigmoid(x):
    return jax.nn.sigmoid(x)

def _layernorm(x, axis=-1, eps=1e-05):
    m = jnp.mean(x, axis=axis, keepdims=True)
    v = jnp.var(x, axis=axis, keepdims=True)
    return (x - m) / jnp.sqrt(v + eps)

def _scatter_add(tgt, idx, src, axis=0):
    return tgt.at[idx].add(src)

def _segment_sum(src, seg, n):
    return jax.ops.segment_sum(src, seg, n)
kernel_name = 'mk_xattn_seq_d2_seqx_r2_630cf9'

def setup_inputs(seed: int=0):
    np.random.seed(seed)
    _w = jnp.asarray

    def _rec_inputs():
        import jax
        import jax.numpy as jnp
        _rk = jax.random.key(seed)
        x = -0.000125 + 0.9999 * jax.random.normal(jax.random.fold_in(_rk, 1), (32, 224, 512), jnp.float32)
        _lenS = 224 - jax.random.randint(jax.random.fold_in(_rk, 7), (32,), 0, max(1, 224 // 4) + 1, jnp.int32)
        _lenS2 = 750 - jax.random.randint(jax.random.fold_in(_rk, 8), (32,), 0, max(1, 750 // 4) + 1, jnp.int32)
        _ctx_512P = jax.random.normal(jax.random.fold_in(_rk, 11), (32, 16, 256), jnp.float32)
        _ctx_512c = jax.random.dirichlet(jax.random.fold_in(_rk, 511), 0.3 * jnp.ones((16,), jnp.float32), (32, 750))
        _ctx_512t = jnp.einsum('bsk,bkd->bsd', _ctx_512c, _ctx_512P)
        _ctx_512t = _ctx_512t * jax.lax.rsqrt(jnp.mean(jnp.square(_ctx_512t)) + 1e-12) * 0.953939
        ctx_512 = 0.000227908 + 0.99994 * (_ctx_512t + 0.3 * jax.random.normal(jax.random.fold_in(_rk, 611), (32, 750, 256), jnp.float32))
        return (x, ctx_512)
    x, ctx_512 = _rec_inputs()

    def _L0_xattn_setup():
        import jax, jax.numpy as jnp
        import numpy as np
        B, T, E = (8, 2048, 512)
        M, L = (128, 256)
        EPS = 1e-06
        key = jax.random.key(seed)
        ks = jax.random.split(key, 5)
        return {'emb': jax.random.normal(ks[0], (B, T, E), dtype=jnp.float32), 'latent': jax.random.normal(ks[1], (B, M, L), dtype=jnp.float32), 'Wq': jax.random.normal(ks[2], (E, E), dtype=jnp.float32) * (1.0 / np.sqrt(E)), 'bq': jnp.zeros((E,), dtype=jnp.float32), 'Wk': jax.random.normal(ks[3], (L, E), dtype=jnp.float32) * (1.0 / np.sqrt(L)), 'bk': jnp.zeros((E,), dtype=jnp.float32), 'Wv': jax.random.normal(ks[4], (L, E), dtype=jnp.float32) * (1.0 / np.sqrt(L)), 'bv': jnp.zeros((E,), dtype=jnp.float32), 'gamma': jnp.ones((E,), dtype=jnp.float32), 'beta': jnp.zeros((E,), dtype=jnp.float32)}
    _L0_xattn_all = _L0_xattn_setup()
    _L0_xattn_in = {k: v for k, v in _L0_xattn_all.items() if k in ('Wq', 'bq', 'Wk', 'bk', 'Wv', 'bv', 'gamma', 'beta')}
    del _L0_xattn_all

    def _L1_xattn_setup():
        import jax, jax.numpy as jnp
        import numpy as np
        B, T, E = (8, 2048, 512)
        M, L = (128, 256)
        EPS = 1e-06
        key = jax.random.key(seed)
        ks = jax.random.split(key, 5)
        return {'emb': jax.random.normal(ks[0], (B, T, E), dtype=jnp.float32), 'latent': jax.random.normal(ks[1], (B, M, L), dtype=jnp.float32), 'Wq': jax.random.normal(ks[2], (E, E), dtype=jnp.float32) * (1.0 / np.sqrt(E)), 'bq': jnp.zeros((E,), dtype=jnp.float32), 'Wk': jax.random.normal(ks[3], (L, E), dtype=jnp.float32) * (1.0 / np.sqrt(L)), 'bk': jnp.zeros((E,), dtype=jnp.float32), 'Wv': jax.random.normal(ks[4], (L, E), dtype=jnp.float32) * (1.0 / np.sqrt(L)), 'bv': jnp.zeros((E,), dtype=jnp.float32), 'gamma': jnp.ones((E,), dtype=jnp.float32), 'beta': jnp.zeros((E,), dtype=jnp.float32)}
    _L1_xattn_all = _L1_xattn_setup()
    _L1_xattn_in = {k: v for k, v in _L1_xattn_all.items() if k in ('Wq', 'bq', 'Wk', 'bk', 'Wv', 'bv', 'gamma', 'beta')}
    del _L1_xattn_all
    return {'x': x, 'ctx_512': ctx_512, 'L0_xattn_Wq': _L0_xattn_in['Wq'], 'L0_xattn_bq': _L0_xattn_in['bq'], 'L0_xattn_Wk': _L0_xattn_in['Wk'], 'L0_xattn_bk': _L0_xattn_in['bk'], 'L0_xattn_Wv': _L0_xattn_in['Wv'], 'L0_xattn_bv': _L0_xattn_in['bv'], 'L0_xattn_gamma': _L0_xattn_in['gamma'], 'L0_xattn_beta': _L0_xattn_in['beta'], 'L1_xattn_Wq': _L1_xattn_in['Wq'], 'L1_xattn_bq': _L1_xattn_in['bq'], 'L1_xattn_Wk': _L1_xattn_in['Wk'], 'L1_xattn_bk': _L1_xattn_in['bk'], 'L1_xattn_Wv': _L1_xattn_in['Wv'], 'L1_xattn_bv': _L1_xattn_in['bv'], 'L1_xattn_gamma': _L1_xattn_in['gamma'], 'L1_xattn_beta': _L1_xattn_in['beta']}

def reference(x, ctx_512, L0_xattn_Wq, L0_xattn_bq, L0_xattn_Wk, L0_xattn_bk, L0_xattn_Wv, L0_xattn_bv, L0_xattn_gamma, L0_xattn_beta, L1_xattn_Wq, L1_xattn_bq, L1_xattn_Wk, L1_xattn_bk, L1_xattn_Wv, L1_xattn_bv, L1_xattn_gamma, L1_xattn_beta):
    import jax
    import jax.numpy as jnp

    def _L0_xattn_ref(emb, latent, Wq, bq, Wk, bk, Wv, bv, gamma, beta):
        import jax, jax.numpy as jnp
        import numpy as np
        B, T, E = (8, 2048, 512)
        M, L = (128, 256)
        EPS = 1e-06
        q = jnp.einsum('bte,ef->btf', emb, Wq) + bq
        k = jnp.einsum('bml,le->bme', latent, Wk) + bk
        v = jnp.einsum('bml,le->bme', latent, Wv) + bv
        scale = 1.0 / jnp.sqrt(jnp.asarray(E, dtype=q.dtype))
        w = jnp.einsum('bte,bme->btm', q, k) * scale
        w = jax.nn.softmax(w, axis=1)
        pred = jnp.einsum('btm,bme->bte', w, v)
        x = pred + emb
        mu = jnp.mean(x, axis=-1, keepdims=True)
        var = jnp.var(x, axis=-1, keepdims=True)
        return (x - mu) * jax.lax.rsqrt(var + EPS) * gamma + beta

    def _L1_xattn_ref(emb, latent, Wq, bq, Wk, bk, Wv, bv, gamma, beta):
        import jax, jax.numpy as jnp
        import numpy as np
        B, T, E = (8, 2048, 512)
        M, L = (128, 256)
        EPS = 1e-06
        q = jnp.einsum('bte,ef->btf', emb, Wq) + bq
        k = jnp.einsum('bml,le->bme', latent, Wk) + bk
        v = jnp.einsum('bml,le->bme', latent, Wv) + bv
        scale = 1.0 / jnp.sqrt(jnp.asarray(E, dtype=q.dtype))
        w = jnp.einsum('bte,bme->btm', q, k) * scale
        w = jax.nn.softmax(w, axis=1)
        pred = jnp.einsum('btm,bme->bte', w, v)
        x = pred + emb
        mu = jnp.mean(x, axis=-1, keepdims=True)
        var = jnp.var(x, axis=-1, keepdims=True)
        return (x - mu) * jax.lax.rsqrt(var + EPS) * gamma + beta
    x = _L0_xattn_ref(x, ctx_512, L0_xattn_Wq, L0_xattn_bq, L0_xattn_Wk, L0_xattn_bk, L0_xattn_Wv, L0_xattn_bv, L0_xattn_gamma, L0_xattn_beta)
    x = _L1_xattn_ref(x, ctx_512, L1_xattn_Wq, L1_xattn_bq, L1_xattn_Wk, L1_xattn_bk, L1_xattn_Wv, L1_xattn_bv, L1_xattn_gamma, L1_xattn_beta)
    return x

_drawn_inputs = setup_inputs


def setup_inputs(seed=0):
    import zlib

    import numpy as np

    out = dict(_drawn_inputs(seed))
    spreads = {'L0_xattn_bq': (0.0, 0.8),
     'L0_xattn_bk': (0.0, 0.432),
     'L0_xattn_bv': (0.0, 0.1),
     'L0_xattn_gamma': (1.0, 0.2),
     'L0_xattn_beta': (0.0, 0.1),
     'L1_xattn_bq': (0.0, 0.8),
     'L1_xattn_bk': (0.0, 0.563),
     'L1_xattn_bv': (0.0, 0.1),
     'L1_xattn_gamma': (1.0, 0.2),
     'L1_xattn_beta': (0.0, 0.1)}
    factors = {}
    for name, (base, spread) in spreads.items():
        noise = np.random.default_rng([zlib.crc32(name.encode()), seed]).standard_normal(out[name].shape)
        drawn = base * np.exp(spread * noise) if base else spread * noise
        out[name] = jnp.asarray(drawn.astype(out[name].dtype))
    for name, factor in factors.items():
        out[name] = (out[name] * factor).astype(out[name].dtype)
    return out
```

```python
from contextlib import ExitStack

import concourse.bass as bass
from concourse import mybir

ALU = mybir.AluOpType
ACT = mybir.ActivationFunctionType
F32 = mybir.dt.float32
F32R = mybir.dt.float32r

LAYERS = 2
EPS = 1e-6
LOOP_SLOTS = 4
UNIT_GAP = 3


def make_schedule(batches):
    last = 2 * (batches - 1) + UNIT_GAP

    def exists(u):
        return 0 <= u <= last and u not in (1, last - 1)

    def count(u):
        return sum(exists(v) for v in range(max(u, -1) + 1))

    class Unit:

        def __init__(self, u, j=None):
            self.u, self.j = u, j
            self.layer = u % 2
            self.batch0 = (u - UNIT_GAP * self.layer) // 2
            self.par = u % 2
            self.slot = self.batch0 % 2

        def at(self, d):
            return Unit(self.u + d, self.j)

        @property
        def real(self):
            return self.j is not None or exists(self.u)

        def n(self, d=0, m=1, add=0):
            if self.j is None:
                return m * count(self.u + d) + add
            return self.j * (LOOP_SLOTS * m) + (m * (self.u + d) + add)

        def past(self, d):
            return self.j is not None or count(self.u + d) > 0

        def pair0(self):
            n = self.u if self.j is not None else count(self.u)
            return (n - 1) % 2

        def batch(self, m=1, add=0):
            b = m * self.batch0 + add
            return b if self.j is None else self.j * (2 * m) + b

        def turns(self, m=1, add=0):
            b = m * (self.batch0 // 2 + 1) + add
            return b if self.j is None else self.j * m + b

    first, end = -1, last + 3
    lo = 2
    hi = (last - 3) // LOOP_SLOTS
    while LOOP_SLOTS * hi > last - 2:
        hi -= 1

    fills = []
    for k in range(first, end):
        ctx_too = k % 2 and 0 <= (k + 1) // 2 < batches
        if ctx_too:
            fills += [(k, "ctx", 0), (k, "ctx", 1)]
        if exists(k + 1):
            fills += [(k, "x", 0), (k, "x", 1)]
        if ctx_too:
            fills += [(k, "ctx", 2)]
        if exists(k + 1):
            fills += [(k, "d", 0)]
    order = {f: n for n, f in enumerate(fills)}

    def fill(k, j, kind, g):
        at = k if j is None else k + LOOP_SLOTS * lo
        n = order[(at, kind, g)]
        if n < 2:
            return n % 2, None
        pk, pkind, pg = fills[n - 2]
        return n % 2, (pk - (at - k), pkind, pg)

    return Unit, exists, fill, (first, lo, hi, end)


def build_xattn(nc, x, ctx, weights, out):
    B, T, E = x.shape
    _, M, L = ctx.shape
    P = 128
    TP, TH = T // 2, 2
    MC = 6
    MP = M // MC
    EC, LC = E // P, L // P
    HALF = MC // 2
    SCALE = float(E) ** -0.5
    assert TP <= P and MP <= P and MP * MC == M and TH * TP == T
    Unit, exists, fill, (FIRST, LO, HI, END) = make_schedule(B)

    with ExitStack() as stack:
        def sb(name, shape, dt=F32):
            return stack.enter_context(nc.sbuf_tensor(name, shape, dt))

        def bank(name):
            return stack.enter_context(nc.psum_tensor(name, [P, 512], F32))

        def sem(name):
            return stack.enter_context(nc.semaphore(name))

        A_hi = sb("A_hi", [P, LAYERS, EC, L], F32R)
        A_lo = sb("A_lo", [P, LAYERS, EC, L], F32R)
        Wv_hi = sb("Wv_hi", [P, LAYERS, LC, E], F32R)
        Wv_lo = sb("Wv_lo", [P, LAYERS, LC, E], F32R)
        c_col = sb("c_col", [P, LAYERS, LC])
        d0_col = sb("d0_col", [P, LAYERS])
        w_row = sb("w_row", [P, LAYERS, E])
        bv_row = sb("bv_row", [P, LAYERS, E])
        gamma_row = sb("gamma_row", [P, LAYERS, E])
        beta_row = sb("beta_row", [P, LAYERS, E])
        bq_col = sb("bq_col", [P, LAYERS, EC])
        bk_col = sb("bk_col", [P, LAYERS, EC])
        bk_wide = sb("bk_wide", [P, LAYERS, EC, P])
        ident = sb("ident", [P, P])
        ones = sb("ones", [P, 2])
        minus_half = sb("minus_half", [P, 1])

        x0 = sb("x0", [P, 2, TH, E])
        x1 = sb("x1", [P, 2, TH, E])
        y_out = sb("y_out", [P, 2, TH, E])
        raw = sb("raw", [P, 2, MC, L])
        cn_hi = sb("cn_hi", [P, 2, MC, L], F32R)
        cn_lo = sb("cn_lo", [P, 2, MC, L], F32R)
        cT_hi = sb("cT_hi", [P, 2, LC, M], F32R)
        cT_lo = sb("cT_lo", [P, 2, LC, M], F32R)

        xT_hi = sb("xT_hi", [P, EC, T], F32R)
        xT_lo = sb("xT_lo", [P, EC, T], F32R)
        qT_hi = sb("qT_hi", [P, LC, T], F32R)
        qT_lo = sb("qT_lo", [P, LC, T], F32R)
        d_col = sb("d_col", [P, TH])
        d_row = sb("d_row", [P, T])
        dot_junk = sb("dot_junk", [P, E])
        scores = sb("scores", [P, MC, T])
        smax = sb("smax", [P, MC])
        neg_max = sb("neg_max", [P, MC])
        ssum = sb("ssum", [P, MC])
        rsum = sb("rsum", [P, MC])
        probs = sb("probs", [P, 2, MC, T])
        pr_hi = sb("pr_hi", [P, 2, MC, T], F32R)
        pr_lo = sb("pr_lo", [P, 2, MC, T], F32R)
        psum3 = sb("psum3", [P, HALF, T])
        psum1 = sb("psum1", [P, T])
        psum_all = sb("psum_all", [P, T])
        oT_hi = sb("oT_hi", [P, LC, T], F32R)
        oT_lo = sb("oT_lo", [P, LC, T], F32R)
        y = sb("y", [P, 2, TH, E])
        z = sb("z", [P, TH, E])
        bn = sb("bn", [P, 2, TH, 6])
        mv = sb("mv", [P, 2, TH, 2])
        ve = sb("ve", [P, 2, TH])
        rstd = sb("rstd", [P, 2, TH])
        nmr = sb("nmr", [P, 2, TH])

        Wq_raw = y[:, :, :, :].rearrange("p a h e -> p (a h) e")
        WqT = y_out[:, :, :, :].rearrange("p a h e -> p (a h) e")
        Wk_raw = x1[:, 0, :, :]
        Wv_raw = x1[:, 1, :, :]
        WkT = scores[:, :, :].rearrange("p c t -> p (c t)")[:, 0:EC * L].rearrange("p (f l) -> p f l", f=EC)

        score_bank = [bank("score_bank0"), bank("score_bank1")]
        t_bank = [bank("t_bank0"), bank("t_bank1")]
        oq_bank = [bank("oq_bank0"), bank("oq_bank1")]
        pv_bank = [bank("pv_bank0"), bank("pv_bank1")]

        def r_psum(u):
            return score_bank[u.at(1).pair0()][0:TP, 0:TH]

        consts_ready = sem("consts_ready")
        w_loaded = [sem("w_loaded0"), sem("w_loaded1")]
        rows_loaded = sem("rows_loaded")
        wT_ready = sem("wT_ready")
        wT_act = sem("wT_act")
        wT_dve = sem("wT_dve")
        fold_ready = sem("fold_ready")
        fold_act = sem("fold_act")
        fold_dve = sem("fold_dve")

        x_loaded = [sem("x_loaded0"), sem("x_loaded1")]
        ctx_loaded = [sem("ctx_loaded0"), sem("ctx_loaded1")]
        stored = [sem("stored0"), sem("stored1")]
        ctxT_ready = sem("ctxT_ready")
        ctxT_hi_done = sem("ctxT_hi_done")
        ctxT_lo_done = sem("ctxT_lo_done")
        cn_hi_done = sem("cn_hi_done")
        cn_done = sem("cn_done")
        xT_ready = sem("xT_ready")
        xT_hi_done = sem("xT_hi_done")
        xT_lo_done = sem("xT_lo_done")
        dot_done = sem("dot_done")
        d_ready = sem("d_ready")
        d_done = sem("d_done")
        q_ready = sem("q_ready")
        qT_hi_done = sem("qT_hi_done")
        qT_lo_done = sem("qT_lo_done")
        s_ready = sem("s_ready")
        smax_done = sem("smax_done")
        neg_max_done = sem("neg_max_done")
        exp_done = sem("exp_done")
        rsum_done = sem("rsum_done")
        probs_done = sem("probs_done")
        pr_hi_done = sem("pr_hi_done")
        pr_lo_done = sem("pr_lo_done")
        psum3_done = sem("psum3_done")
        psum1_done = sem("psum1_done")
        psum_done = sem("psum_done")
        o_ready = sem("o_ready")
        oT_hi_done = sem("oT_hi_done")
        oT_lo_done = sem("oT_lo_done")
        r_ready = sem("r_ready")
        resid_done = sem("resid_done")
        pv_ready = sem("pv_ready")
        y_done = sem("y_done")
        bn_done = sem("bn_done")
        mv_done = sem("mv_done")
        ve_done = sem("ve_done")
        rstd_done = sem("rstd_done")
        nmr_done = sem("nmr_done")
        z_done = sem("z_done")
        zg_done = sem("zg_done")
        ln_done = sem("ln_done")

        wait_alone = sem("wait_alone")

        block = stack.enter_context(nc.Block())

        def slots(eng, slot):
            for k in range(FIRST, LOOP_SLOTS * LO):
                slot(k, None)
            with eng.Fori(LO, HI) as j:
                for s in range(LOOP_SLOTS):
                    slot(s, j)
            for k in range(LOOP_SLOTS * HI, END):
                slot(k, None)

        def batch_of_ctx(k, j):
            u = Unit(k + 1, j)
            return u if k % 2 and u.real and u.layer == 0 else None

        @block.sync
        def _(sp):
            for l in range(LAYERS):
                W = weights[l]
                if l > 0:
                    sp.wait_ge(wT_ready, 6 * l)
                    sp.wait_ge(fold_act, 3 * l)
                    sp.wait_ge(fold_dve, 6 * l)
                sp.dma_start(Wq_raw, W["Wq"].rearrange("(c p) f -> p c f", p=P)).then_inc(w_loaded[l], 16)
                sp.dma_start(Wk_raw, W["Wk"].rearrange("(c p) f -> p c f", p=P)).then_inc(w_loaded[l], 16)
                sp.dma_start(Wv_raw, W["Wv"].rearrange("(c p) e -> p c e", p=P)).then_inc(w_loaded[l], 16)
                if l == 0:
                    for i in range(2):
                        sp.dma_start(x0[0:TP, i], x[i].rearrange("(p h) e -> p h e", h=TH)).then_inc(x_loaded[i], 16)
                        sp.dma_start(raw[0:MP, i], ctx[i].rearrange("(p c) l -> p c l", c=MC)).then_inc(ctx_loaded[i], 16)

            def slot(k, j):
                if k % 2 == 0:
                    return
                done, nxt = Unit(k - 2, j), Unit(k + 3, j)
                if done.real:
                    sp.wait_ge(ln_done, done.n(m=2))
                    sp.sem_inc(wait_alone, 1)
                    sp.dma_start(out[done.batch()].rearrange("(p h) e -> p h e", h=TH),
                                 y_out[0:TP, done.slot]).then_inc(stored[done.slot], 16)
                if nxt.real and k >= 1:
                    sp.wait_ge(resid_done, nxt.n(-4, 2))
                    sp.sem_inc(wait_alone, 1)
                    sp.dma_start(x0[0:TP, nxt.slot],
                                 x[nxt.batch()].rearrange("(p h) e -> p h e", h=TH)).then_inc(x_loaded[nxt.slot], 16)
                    sp.wait_ge(cn_done, nxt.batch(2, -2))
                    sp.sem_inc(wait_alone, 1)
                    sp.dma_start(raw[0:MP, nxt.slot],
                                 ctx[nxt.batch()].rearrange("(p c) l -> p c l", c=MC)).then_inc(ctx_loaded[nxt.slot], 16)

            slots(sp, slot)
            for i in range(2):
                sp.wait_ge(stored[i], 16 * (B // 2))

        @block.tensor
        def _(pe):
            pe.wait_ge(consts_ready, 4)
            for l in range(LAYERS):
                pe.wait_ge(w_loaded[l], 16 * 5)
                if l > 0:
                    pe.wait_ge(fold_act, 3 * l)
                    pe.wait_ge(fold_dve, 6 * l)
                for f, b in enumerate(t_bank + pv_bank):
                    for e in range(EC):
                        ins = nc.tensor.transpose(b[:, e * P:(e + 1) * P], Wq_raw[:, e, f * P:(f + 1) * P], ident[:, :])
                    ins.then_inc(wT_ready, 1)
                for g, b in enumerate(score_bank):
                    for f in range(2):
                        for c in range(LC):
                            at = f * L + c * P
                            ff = 2 * g + f
                            ins = nc.tensor.transpose(b[:, at:at + P], Wk_raw[:, c, ff * P:(ff + 1) * P], ident[:, :])
                    ins.then_inc(wT_ready, 1)
                pe.wait_ge(wT_act, 4 * (l + 1))
                pe.wait_ge(wT_dve, 3 * (l + 1))
                for g, b in enumerate(oq_bank):
                    for e in range(2):
                        ee = 2 * g + e
                        for f in range(EC):
                            ins = nc.tensor.matmul(b[:, e * L:(e + 1) * L], WqT[:, f, ee * P:(ee + 1) * P], WkT[:, f, :],
                                                   start=(f == 0), stop=(f == EC - 1))
                    ins.then_inc(fold_ready, 1)
                for f in range(EC):
                    ins = nc.tensor.matmul(t_bank[0][:, 0:E], bk_wide[:, l, f, :], WqT[:, f, :],
                                           start=(f == 0), stop=(f == EC - 1))
                ins.then_inc(fold_ready, 1)
                for c in range(LC):
                    for f in range(EC):
                        nc.tensor.matmul(t_bank[1][:, c:c + 1], WkT[:, f, c * P:(c + 1) * P], bq_col[:, l, f:f + 1],
                                         start=(f == 0), stop=(f == EC - 1))
                for f in range(EC):
                    ins = nc.tensor.matmul(t_bank[1][:, LC:LC + 1], bk_wide[:, l, f, :], bq_col[:, l, f:f + 1],
                                           start=(f == 0), stop=(f == EC - 1))
                ins.then_inc(fold_ready, 1)
            pe.wait_ge(fold_act, 3 * LAYERS)
            pe.wait_ge(fold_dve, 6 * LAYERS)

            def bank_free(k, j, kind, g):
                b, before = fill(k, j, kind, g)
                if before:
                    pk, pkind, pg = before
                    u = Unit(pk + 1, j)
                    if pkind == "x":
                        pe.wait_ge(xT_lo_done, u.n(m=2, add=pg - 1))
                    elif pkind == "ctx":
                        pe.wait_ge(ctxT_lo_done, u.batch(3, pg + 1))
                    else:
                        pe.wait_ge(d_done, u.n())
                return t_bank[b]

            def transpose_ctx(k, j, g):
                u = batch_of_ctx(k, j)
                if u is None:
                    return
                if g == 0:
                    pe.wait_ge(ctx_loaded[u.slot], u.turns(16))
                b = bank_free(k, j, "ctx", g)
                for l in range(LC):
                    for c in range(2):
                        at = (l * 2 + c) * MP
                        ins = nc.tensor.transpose(b[:, at:at + MP], raw[0:MP, u.slot, 2 * g + c, l * P:(l + 1) * P],
                                                  ident[0:MP, 0:MP])
                ins.then_inc(ctxT_ready, 1)

            def transpose_x(k, j, g):
                u = Unit(k + 1, j)
                if g == 0:
                    if u.layer == 0:
                        pe.wait_ge(x_loaded[u.slot], u.turns(16))
                    else:
                        pe.wait_ge(ln_done, u.n(-UNIT_GAP, 2))
                b = bank_free(k, j, "x", g)
                src = (x0, x1)[u.layer]
                for e in range(2):
                    for h in range(TH):
                        at = e * T + h * TP
                        ee = 2 * g + e
                        ins = nc.tensor.transpose(b[:, at:at + TP], src[0:TP, u.slot, h, ee * P:(ee + 1) * P],
                                                  ident[0:TP, 0:TP])
                ins.then_inc(xT_ready, 1)

            def spread_d(k, j):
                u = Unit(k + 1, j)
                pe.wait_ge(dot_done, u.n(m=2))
                b = bank_free(k, j, "d", 0)
                for h in range(TH):
                    ins = nc.tensor.transpose(b[:, h * TP:(h + 1) * TP], d_col[0:TP, h:h + 1].to_broadcast([TP, P]),
                                              ident[0:TP, 0:TP])
                ins.then_inc(d_ready, 1)

            def q_product(u):
                for l in range(LC):
                    for e in range(EC):
                        if l == 0 and e % 2 == 0:
                            pe.wait_ge(xT_hi_done, u.n(m=2, add=e // 2 - 1))
                            pe.wait_ge(xT_lo_done, u.n(m=2, add=e // 2 - 1))
                        hi = A_hi[:, u.layer, e, l * P:(l + 1) * P]
                        lo = A_lo[:, u.layer, e, l * P:(l + 1) * P]
                        o = oq_bank[l][:, 0:T]
                        nc.tensor.matmul(o, hi, xT_hi[:, e, :], start=(e == 0), stop=False)
                        nc.tensor.matmul(o, hi, xT_lo[:, e, :], start=False, stop=False)
                        ins = nc.tensor.matmul(o, lo, xT_hi[:, e, :], start=False, stop=(e == EC - 1))
                    ins.then_inc(q_ready, 1)

            def score_product(u):
                pe.wait_ge(qT_hi_done, u.n(m=2))
                pe.wait_ge(qT_lo_done, u.n(m=2))
                for p in range(MC // 2):
                    if u.layer == 0:
                        pe.wait_ge(ctxT_hi_done, u.batch(3, p + 1))
                        pe.wait_ge(ctxT_lo_done, u.batch(3, p + 1))
                    if u.past(-1) or p == 2:
                        pe.wait_ge(smax_done, u.n(m=6, add=2 * p - 8))
                    if p == 1 and u.past(-2):
                        pe.wait_ge(resid_done, u.n(-2, 2))
                    b = score_bank[(u.pair0() + p) % 2]
                    for c in range(2):
                        cols = slice((2 * p + c) * MP, (2 * p + c + 1) * MP)
                        o = b[0:MP, c * T:(c + 1) * T]
                        for l in range(LC):
                            hi, lo = cT_hi[:, u.slot, l, cols], cT_lo[:, u.slot, l, cols]
                            nc.tensor.matmul(o, hi, qT_hi[:, l, :], start=(l == 0), stop=False)
                            nc.tensor.matmul(o, hi, qT_lo[:, l, :], start=False, stop=False)
                            ins = nc.tensor.matmul(o, lo, qT_hi[:, l, :], start=False, stop=(l == LC - 1))
                    ins.then_inc(s_ready, 1)

            def o_product(u, l):
                if l == 0:
                    pe.wait_ge(pr_lo_done, u.n(m=2))
                    pe.wait_ge(pr_hi_done, u.n(m=2))
                if u.layer == 0:
                    pe.wait_ge(cn_done, u.batch(2, l + 1))
                o = oq_bank[l][:, 0:T]
                for c in range(MC):
                    hi = cn_hi[0:MP, u.slot, c, l * P:(l + 1) * P]
                    lo = cn_lo[0:MP, u.slot, c, l * P:(l + 1) * P]
                    nc.tensor.matmul(o, hi, pr_hi[0:MP, u.par, c, :], start=(c == 0), stop=False)
                    nc.tensor.matmul(o, hi, pr_lo[0:MP, u.par, c, :], start=False, stop=False)
                    ins = nc.tensor.matmul(o, lo, pr_hi[0:MP, u.par, c, :], start=False, stop=(c == MC - 1))
                ins.then_inc(o_ready, 1)

            def r_product(u):
                pe.wait_ge(psum_done, u.n())
                pe.wait_ge(smax_done, u.n(1, 6))
                for h in range(TH):
                    ins = nc.tensor.matmul(r_psum(u)[:, h:h + 1], psum_all[0:MP, h * TP:(h + 1) * TP], ones[0:MP, 0:1],
                                           start=True, stop=True)
                ins.then_inc(r_ready, 1)

            def pv_product(u, h):
                if u.past(-1):
                    pe.wait_ge(y_done, u.n(-1, 2, h - 1))
                o = pv_bank[h][0:TP, :]
                for l in range(LC):
                    if h == 0:
                        pe.wait_ge(oT_hi_done, u.n(m=2, add=l - 1))
                        pe.wait_ge(oT_lo_done, u.n(m=2, add=l - 1))
                    rows = slice(h * TP, (h + 1) * TP)
                    hi, lo = oT_hi[:, l, rows], oT_lo[:, l, rows]
                    nc.tensor.matmul(o, hi, Wv_hi[:, u.layer, l, :], start=(l == 0), stop=False)
                    nc.tensor.matmul(o, hi, Wv_lo[:, u.layer, l, :], start=False, stop=False)
                    ins = nc.tensor.matmul(o, lo, Wv_hi[:, u.layer, l, :], start=False, stop=(l == LC - 1))
                ins.then_inc(pv_ready, 1)

            def slot(k, j):
                now, last, nxt = Unit(k, j), Unit(k - 1, j), Unit(k + 1, j)
                if now.real:
                    score_product(now)
                transpose_ctx(k, j, 0)
                if last.real:
                    o_product(last, 0)
                    r_product(last)
                transpose_ctx(k, j, 1)
                if last.real:
                    o_product(last, 1)
                if nxt.real:
                    transpose_x(k, j, 0)
                    transpose_x(k, j, 1)
                if last.real:
                    pv_product(last, 0)
                if nxt.real:
                    q_product(nxt)
                transpose_ctx(k, j, 2)
                if last.real:
                    pv_product(last, 1)
                if nxt.real:
                    spread_d(k, j)

            slots(pe, slot)

        @block.scalar
        def _(act):
            for l in range(LAYERS):
                W = weights[l]
                act.dma_start(bq_col[:, l, :], W["bq"].rearrange("(c p) -> p c", p=P),
                              allow_slow_non_contiguous=True).then_inc(w_loaded[l], 16)
                act.dma_start(bk_col[:, l, :], W["bk"].rearrange("(c p) -> p c", p=P),
                              allow_slow_non_contiguous=True).then_inc(w_loaded[l], 16)
                act.dma_start(bv_row[:, l, :], W["bv"].partition_broadcast(P)).then_inc(rows_loaded, 16)
                act.dma_start(gamma_row[:, l, :], W["gamma"].partition_broadcast(P)).then_inc(rows_loaded, 16)
                act.dma_start(beta_row[:, l, :], W["beta"].partition_broadcast(P)).then_inc(rows_loaded, 16)
            for l in range(LAYERS):
                act.wait_ge(w_loaded[l], 16 * 5)
                act.activation(Wv_hi[:, l, :, :], Wv_raw, ACT.Identity).then_inc(fold_act, 1)
                for f, b in enumerate(t_bank + pv_bank):
                    act.wait_ge(wT_ready, 6 * l + f + 1)
                    act.activation(WqT[:, f, :], b[:, :], ACT.Identity).then_inc(wT_act, 1)
                for g, b in enumerate(oq_bank):
                    act.wait_ge(fold_ready, 4 * l + g + 1)
                    act.activation(A_hi[:, l, 2 * g:2 * g + 2, :], b[:, :].rearrange("p (e l) -> p e l", e=2),
                                   ACT.Identity).then_inc(fold_act, 1)

            def ctxT_hi(k, j, g):
                u = batch_of_ctx(k, j)
                if u is None:
                    return
                act.wait_ge(ctxT_ready, u.batch(3, g + 1))
                b = t_bank[fill(k, j, "ctx", g)[0]]
                act.activation(cT_hi[:, u.slot, :, 2 * g * MP:(2 * g + 2) * MP],
                               b[:, 0:4 * MP].rearrange("p (l m) -> p l m", l=LC), ACT.Identity).then_inc(ctxT_hi_done, 1)

            def ctx_hi(u, l):
                cols = slice(l * P, (l + 1) * P)
                if l == 0:
                    act.wait_ge(ctx_loaded[u.slot], u.turns(16))
                if u.past(-1):
                    act.wait_ge(o_ready, u.n(-1, 2, l - 1))
                act.activation(cn_hi[0:MP, u.slot, :, cols], raw[0:MP, u.slot, :, cols], ACT.Identity).then_inc(cn_hi_done, 1)

            def xT_hi_part(k, j, g):
                u = Unit(k + 1, j)
                act.wait_ge(xT_ready, u.n(m=2, add=g - 1))
                if u.past(-1) and g == 0:
                    act.wait_ge(q_ready, u.n(-1, 2))
                b = t_bank[fill(k, j, "x", g)[0]]
                act.activation(xT_hi[:, 2 * g:2 * g + 2, :], b[:, 0:2 * T].rearrange("p (e t) -> p e t", e=2),
                               ACT.Identity).then_inc(xT_hi_done, 1)

            def d_out(k, j):
                u = Unit(k + 1, j)
                act.wait_ge(d_ready, u.n())
                if u.past(-1):
                    act.wait_ge(smax_done, u.n(-1, 6))
                act.activation(d_row[:, :], t_bank[fill(k, j, "d", 0)[0]][:, 0:T], ACT.Identity).then_inc(d_done, 1)

            def q_hi(u, l):
                act.wait_ge(q_ready, u.n(m=2, add=l - 1))
                if u.past(-1) and l == 0:
                    act.wait_ge(s_ready, u.n(-1, 3))
                act.activation(qT_hi[:, l, :], oq_bank[l][:, 0:T], ACT.Identity,
                               bias=c_col[:, u.layer, l:l + 1]).then_inc(qT_hi_done, 1)

            def exps(u, half):
                act.wait_ge(neg_max_done, u.n(m=2, add=half - 1))
                if u.past(-2) and half == 0:
                    act.wait_ge(pr_lo_done, u.n(-2, 2))
                    act.wait_ge(psum3_done, u.n(-2))
                for c in range(HALF * half, HALF * (half + 1)):
                    ins = act.activation(probs[0:MP, u.par, c, :], scores[0:MP, c, :], ACT.Exp,
                                         bias=neg_max[0:MP, c:c + 1], scale=SCALE, accum_out=ssum[0:MP, c:c + 1])
                ins.then_inc(exp_done, 1)

            def normalise(u, half):
                act.wait_ge(rsum_done, u.n(m=2, add=half - 1))
                for c in range(HALF * half, HALF * (half + 1)):
                    ins = act.activation(probs[0:MP, u.par, c, :], probs[0:MP, u.par, c, :], ACT.Identity,
                                         scale=rsum[0:MP, c:c + 1])
                ins.then_inc(probs_done, 1)

            def probs_hi(u, half):
                chunks = slice(HALF * half, HALF * (half + 1))
                act.wait_ge(probs_done, u.n(m=2, add=half - 1))
                if u.past(-2) and half == 0:
                    act.wait_ge(o_ready, u.n(-2, 2))
                act.activation(pr_hi[0:MP, u.par, chunks, :], probs[0:MP, u.par, chunks, :], ACT.Identity).then_inc(pr_hi_done, 1)

            def o_hi(u, l):
                act.wait_ge(o_ready, u.n(m=2, add=l - 1))
                if u.past(-1) and l == 0:
                    act.wait_ge(pv_ready, u.n(-1, 2))
                act.activation(oT_hi[:, l, :], oq_bank[l][:, 0:T], ACT.Identity).then_inc(oT_hi_done, 1)

            def standardise(u, h):
                act.wait_ge(nmr_done, u.n(m=2, add=h - 1))
                if u.past(-1):
                    act.wait_ge(ln_done, u.n(-1, 2, h - 1))
                act.activation(z[0:TP, h, :], y[0:TP, u.par, h, :], ACT.Identity, bias=nmr[0:TP, u.par, h:h + 1],
                               scale=rstd[0:TP, u.par, h:h + 1]).then_inc(z_done, 1)

            def slot(k, j):
                now, last, prev, nxt = Unit(k, j), Unit(k - 1, j), Unit(k - 2, j), Unit(k + 1, j)
                if prev.real and prev.layer == 0:
                    standardise(prev, 1)
                if now.real:
                    exps(now, 0)
                ctxT_hi(k, j, 0)
                if now.real:
                    exps(now, 1)
                if last.real:
                    o_hi(last, 0)
                ctxT_hi(k, j, 1)
                if k % 2 == 0 and now.real:
                    ctx_hi(now, 0)
                if last.real:
                    o_hi(last, 1)
                if nxt.real:
                    xT_hi_part(k, j, 0)
                    xT_hi_part(k, j, 1)
                if now.real:
                    normalise(now, 0)
                    probs_hi(now, 0)
                if prev.real and prev.layer == 1:
                    standardise(prev, 1)
                if nxt.real:
                    q_hi(nxt, 0)
                if now.real:
                    normalise(now, 1)
                if nxt.real:
                    q_hi(nxt, 1)
                ctxT_hi(k, j, 2)
                if now.real:
                    probs_hi(now, 1)
                if nxt.real:
                    d_out(k, j)
                if last.real:
                    standardise(last, 0)
                if k % 2 == 0 and now.real:
                    ctx_hi(now, 1)

            slots(act, slot)

        @block.vector
        def _(dve):
            for l in range(LAYERS):
                dve.wait_ge(w_loaded[l], 16 * 5)
                dve.tensor_copy(bk_wide[:, l, :, :], bk_col[:, l, :].unsqueeze(2).to_broadcast([P, EC, P])).then_inc(wT_dve, 1)
                dve.wait_ge(fold_act, 3 * l + 1)
                dve.tensor_tensor(Wv_lo[:, l, :, :], Wv_raw, Wv_hi[:, l, :, :].bitcast(F32), ALU.subtract).then_inc(fold_dve, 1)
                for g, b in enumerate(score_bank):
                    dve.wait_ge(wT_ready, 6 * l + 4 + g + 1)
                    dve.tensor_copy(WkT[:, 2 * g:2 * g + 2, :], b[:, :].rearrange("p (f l) -> p f l", f=2)).then_inc(wT_dve, 1)
                for g, b in enumerate(oq_bank):
                    dve.wait_ge(fold_act, 3 * l + g + 2)
                    dve.tensor_tensor(A_lo[:, l, 2 * g:2 * g + 2, :], b[:, :].rearrange("p (e l) -> p e l", e=2),
                                      A_hi[:, l, 2 * g:2 * g + 2, :].bitcast(F32), ALU.subtract).then_inc(fold_dve, 1)
                dve.wait_ge(fold_ready, 4 * l + 4)
                dve.tensor_copy(w_row[:, l, :], t_bank[0][:, 0:E]).then_inc(fold_dve, 1)
                dve.tensor_copy(c_col[:, l, :], t_bank[1][:, 0:LC]).then_inc(fold_dve, 1)
                dve.tensor_copy(d0_col[:, l:l + 1], t_bank[1][:, LC:LC + 1]).then_inc(fold_dve, 1)
            dve.wait_ge(fold_dve, 6 * LAYERS)
            dve.wait_ge(rows_loaded, 16 * 3 * LAYERS)

            def ctxT_lo(k, j, g):
                u = batch_of_ctx(k, j)
                if u is None:
                    return
                dve.wait_ge(ctxT_hi_done, u.batch(3, g + 1))
                b = t_bank[fill(k, j, "ctx", g)[0]]
                cols = slice(2 * g * MP, (2 * g + 2) * MP)
                dve.tensor_tensor(cT_lo[:, u.slot, :, cols], b[:, 0:4 * MP].rearrange("p (l m) -> p l m", l=LC),
                                  cT_hi[:, u.slot, :, cols].bitcast(F32), ALU.subtract).then_inc(ctxT_lo_done, 1)

            def xT_lo_part(k, j, g):
                u = Unit(k + 1, j)
                dve.wait_ge(xT_hi_done, u.n(m=2, add=g - 1))
                b = t_bank[fill(k, j, "x", g)[0]]
                dve.tensor_tensor(xT_lo[:, 2 * g:2 * g + 2, :], b[:, 0:2 * T].rearrange("p (e t) -> p e t", e=2),
                                  xT_hi[:, 2 * g:2 * g + 2, :].bitcast(F32), ALU.subtract).then_inc(xT_lo_done, 1)

            def dot(u, h):
                if h == 0:
                    if u.layer == 0:
                        dve.wait_ge(x_loaded[u.slot], u.turns(16))
                    else:
                        dve.wait_ge(ln_done, u.n(-UNIT_GAP, 2))
                    if u.past(-1):
                        dve.wait_ge(d_ready, u.n(-1))
                if u.past(-1) or h:
                    dve.wait_ge(dot_done, u.n(m=2, add=h - 2))
                dve.tensor_tensor_reduce(dot_junk[0:TP, :], (x0, x1)[u.layer][0:TP, u.slot, h, :], w_row[0:TP, u.layer, :], 1.0,
                                         d0_col[0:TP, u.layer:u.layer + 1], ALU.mult, ALU.add,
                                         d_col[0:TP, h:h + 1]).then_inc(dot_done, 1)

            def q_lo(u, l):
                dve.wait_ge(qT_hi_done, u.n(m=2, add=l - 1))
                dve.scalar_tensor_tensor(out=qT_lo[:, l, :], in0=oq_bank[l][:, 0:T],
                                         scalar=c_col[:, u.layer, l:l + 1], in1=qT_hi[:, l, :].bitcast(F32),
                                         op0=ALU.add, op1=ALU.subtract).then_inc(qT_lo_done, 1)

            def score_max(u, c):
                if c == 0:
                    dve.wait_ge(d_done, u.n())
                    if u.past(-1):
                        dve.wait_ge(exp_done, u.n(-1, 2))
                if c % 2 == 0:
                    dve.wait_ge(s_ready, u.n(m=3, add=c // 2 - 2))
                    dve.sem_inc(wait_alone, 1)
                b = score_bank[(u.pair0() + c // 2) % 2]
                dve.tensor_tensor_reduce(scores[0:MP, c, :], b[0:MP, (c % 2) * T:(c % 2 + 1) * T], d_row[0:MP, :], 1.0,
                                         -3.4e38, ALU.add, ALU.max, smax[0:MP, c:c + 1]).then_inc(smax_done, 1)

            def negate_max(u, half):
                cols = slice(HALF * half, HALF * (half + 1))
                dve.wait_ge(smax_done, u.n(m=6, add=HALF * (half + 1) - 6))
                dve.tensor_scalar(neg_max[0:MP, cols], smax[0:MP, cols], -SCALE, None, ALU.mult).then_inc(neg_max_done, 1)

            def invert_sum(u, half):
                cols = slice(HALF * half, HALF * (half + 1))
                dve.wait_ge(exp_done, u.n(m=2, add=half - 1))
                dve.reciprocal(rsum[0:MP, cols], ssum[0:MP, cols]).then_inc(rsum_done, 1)

            def probs_lo(u, half):
                chunks = slice(HALF * half, HALF * (half + 1))
                dve.wait_ge(pr_hi_done, u.n(m=2, add=half - 1))
                dve.tensor_tensor(pr_lo[0:MP, u.par, chunks, :], probs[0:MP, u.par, chunks, :],
                                  pr_hi[0:MP, u.par, chunks, :].bitcast(F32), ALU.subtract).then_inc(pr_lo_done, 1)

            def o_lo(u, l):
                dve.wait_ge(oT_hi_done, u.n(m=2, add=l - 1))
                dve.tensor_tensor(oT_lo[:, l, :], oq_bank[l][:, 0:T], oT_hi[:, l, :].bitcast(F32),
                                  ALU.subtract).then_inc(oT_lo_done, 1)

            def residual(u, h):
                if h == 0:
                    dve.wait_ge(r_ready, u.n())
                if u.past(-2):
                    dve.wait_ge(z_done, u.n(-2, 2, h - 1))
                dve.scalar_tensor_tensor(out=y[0:TP, u.par, h, :], in0=bv_row[0:TP, u.layer, :], scalar=r_psum(u)[:, h:h + 1],
                                         in1=(x0, x1)[u.layer][0:TP, u.slot, h, :],
                                         op0=ALU.mult, op1=ALU.add).then_inc(resid_done, 1)

            def add_pv(u, h):
                dve.wait_ge(pv_ready, u.n(m=2, add=h - 1))
                dve.wait_ge(resid_done, u.n(m=2, add=h - 1))
                dve.tensor_tensor(y[0:TP, u.par, h, :], pv_bank[h][0:TP, :], y[0:TP, u.par, h, :], ALU.add).then_inc(y_done, 1)
                dve.wait_ge(y_done, u.n(m=2, add=h - 1))
                dve.bn_stats(bn[0:TP, u.par, h, :], y[0:TP, u.par, h, :]).then_inc(bn_done, 1)

            def moments(u, h):
                dve.wait_ge(bn_done, u.n(m=2, add=h - 1))
                dve.sem_inc(wait_alone, 1)
                dve.bn_aggr(mv[0:TP, u.par, h, :], bn[0:TP, u.par, h, :]).then_inc(mv_done, 1)
                dve.wait_ge(mv_done, u.n(m=2, add=h - 1))
                dve.tensor_scalar(ve[0:TP, u.par, h:h + 1], mv[0:TP, u.par, h, 1:2], EPS, None, ALU.add).then_inc(ve_done, 1)

            def shift(u, h):
                dve.wait_ge(rstd_done, u.n(m=2, add=h - 1))
                dve.scalar_tensor_tensor(out=nmr[0:TP, u.par, h:h + 1], in0=mv[0:TP, u.par, h, 0:1], scalar=-1.0,
                                         in1=rstd[0:TP, u.par, h:h + 1], op0=ALU.mult, op1=ALU.mult).then_inc(nmr_done, 1)

            def slot(k, j):
                now, last, prev, nxt = Unit(k, j), Unit(k - 1, j), Unit(k - 2, j), Unit(k + 1, j)
                if prev.real:
                    add_pv(prev, 1)
                if now.real:
                    score_max(now, 0)
                    score_max(now, 1)
                if prev.real:
                    moments(prev, 1)
                if now.real:
                    score_max(now, 2)
                    negate_max(now, 0)
                    score_max(now, 3)
                if prev.real and prev.layer == 0:
                    shift(prev, 1)
                if now.real:
                    score_max(now, 4)
                    score_max(now, 5)
                    negate_max(now, 1)
                ctxT_lo(k, j, 0)
                if now.real:
                    invert_sum(now, 0)
                if last.real:
                    residual(last, 0)
                    o_lo(last, 0)
                if now.real:
                    invert_sum(now, 1)
                if last.real:
                    residual(last, 1)
                ctxT_lo(k, j, 1)
                if last.real:
                    o_lo(last, 1)
                if nxt.real:
                    xT_lo_part(k, j, 0)
                    xT_lo_part(k, j, 1)
                if prev.real and prev.layer == 1:
                    shift(prev, 1)
                if last.real:
                    add_pv(last, 0)
                if nxt.real:
                    dot(nxt, 0)
                    q_lo(nxt, 0)
                    dot(nxt, 1)
                if last.real:
                    moments(last, 0)
                if now.real:
                    probs_lo(now, 0)
                if nxt.real:
                    q_lo(nxt, 1)
                ctxT_lo(k, j, 2)
                if now.real:
                    probs_lo(now, 1)
                if last.real:
                    shift(last, 0)

            slots(dve, slot)

        @block.gpsimd
        def _(pool):
            pool.memset(ident[:, :], 0.0).then_inc(consts_ready, 1)
            pool.memset(ones[:, :], 1.0).then_inc(consts_ready, 1)
            pool.memset(minus_half[:, :], -0.5).then_inc(consts_ready, 1)
            pool.wait_ge(consts_ready, 3)
            pool.affine_select(out=ident[:, :], in_=ident[:, :], compare_op=ALU.not_equal, fill=1.0, base=0,
                               pattern=[[-1, P]], channel_multiplier=1).then_inc(consts_ready, 1)
            pool.wait_ge(consts_ready, 4)
            pool.wait_ge(rows_loaded, 16 * 3 * LAYERS)

            def ctx_lo(u, l):
                cols = slice(l * P, (l + 1) * P)
                pool.wait_ge(cn_hi_done, u.batch(2, l + 1))
                pool.tensor_tensor(cn_lo[0:MP, u.slot, :, cols], raw[0:MP, u.slot, :, cols],
                                   cn_hi[0:MP, u.slot, :, cols].bitcast(F32), ALU.subtract).then_inc(cn_done, 1)

            def sum_probs(u):
                pool.wait_ge(probs_done, u.n(m=2))
                pool.tensor_tensor(psum3[0:MP, :, :], probs[0:MP, u.par, 0:HALF, :], probs[0:MP, u.par, HALF:MC, :],
                                   ALU.add).then_inc(psum3_done, 1)
                pool.wait_ge(psum3_done, u.n())
                pool.tensor_tensor(psum1[0:MP, :], psum3[0:MP, 0, :], psum3[0:MP, 1, :], ALU.add).then_inc(psum1_done, 1)
                pool.wait_ge(psum1_done, u.n())
                if u.past(-1):
                    pool.wait_ge(r_ready, u.n(-1))
                pool.tensor_tensor(psum_all[0:MP, :], psum1[0:MP, :], psum3[0:MP, 2, :], ALU.add).then_inc(psum_done, 1)

            def inverse_deviation(u, h):
                pool.wait_ge(ve_done, u.n(m=2, add=h - 1))
                pool.tensor_tensor(rstd[0:TP, u.par, h:h + 1], ve[0:TP, u.par, h:h + 1], minus_half[0:TP, :],
                                   ALU.pow).then_inc(rstd_done, 1)

            def scale_shift(u, h):
                pool.wait_ge(z_done, u.n(m=2, add=h - 1))
                pool.tensor_tensor(z[0:TP, h, :], z[0:TP, h, :], gamma_row[0:TP, u.layer, :], ALU.mult).then_inc(zg_done, 1)
                pool.wait_ge(zg_done, u.n(m=2, add=h - 1))
                if u.layer == 0:
                    if u.past(-1):
                        pool.wait_ge(resid_done, u.n(-1, 2))
                        pool.wait_ge(q_ready, u.n(-1, 2))
                        pool.wait_ge(d_ready, u.n(-1))
                    dst = x1
                else:
                    if u.j is not None or u.batch0 >= 2:
                        pool.wait_ge(stored[u.slot], u.turns(16, -16))
                    dst = y_out
                pool.tensor_tensor(dst[0:TP, u.slot, h, :], z[0:TP, h, :], beta_row[0:TP, u.layer, :], ALU.add).then_inc(ln_done, 1)

            def slot(k, j):
                now, last, prev = Unit(k, j), Unit(k - 1, j), Unit(k - 2, j)
                if k % 2 and last.real:
                    ctx_lo(last, 1)
                if prev.real:
                    scale_shift(prev, 0)
                    inverse_deviation(prev, 1)
                    scale_shift(prev, 1)
                if k % 2 == 0 and now.real:
                    ctx_lo(now, 0)
                if last.real:
                    inverse_deviation(last, 0)
                if now.real:
                    sum_probs(now)

            slots(pool, slot)


_NAMES = ("Wq", "bq", "Wk", "bk", "Wv", "bv", "gamma", "beta")


def kernel(**inputs):
    import numpy as _np
    import concourse.bacc as _bacc
    from concourse import mybir as _mybir
    from concourse.bass_utils import run_bass_kernel_spmd as _run

    nc = _bacc.Bacc("TRN2", target_bir_lowering=False, num_devices=1)
    arrays = {}

    def given(name):
        a = _np.ascontiguousarray(inputs[name])
        arrays[f"in_{name}_dram"] = a
        return nc.dram_tensor(f"in_{name}_dram", a.shape, _mybir.dt.from_np(a.dtype), kind="ExternalInput").ap()

    x = given("x")
    ctx = given("ctx_512")
    weights = [{n: given(f"L{l}_xattn_{n}") for n in _NAMES} for l in range(LAYERS)]
    out = nc.dram_tensor("out_0_dram", x.shape, _mybir.dt.float32, kind="ExternalOutput").ap()
    build_xattn(nc, x, ctx, weights, out)
    r = _run(nc, [arrays], core_ids=[0])
    return r.results[0]["out_0_dram"]
```

```python
from contextlib import ExitStack

import concourse.bass as bass
from concourse import mybir

ALU = mybir.AluOpType
ACT = mybir.ActivationFunctionType
F32 = mybir.dt.float32
F32R = mybir.dt.float32r

LAYERS = 2
EPS = 1e-6
LOOP_SLOTS = 4
R_HALF = 1
UNIT_GAP = 3
START_FILLS = [("X", 0), ("X", 1), ("C", 0), ("C", 1), ("C", 2), ("D", 0)]
SLOT_FILLS = [
    [("C", 2, 0), ("X", 0, 1), ("X", 1, 1)],
    [("D", 0, 0), ("C", 0, 1), ("C", 1, 1), ("X", 0, 1), ("X", 1, 1), ("D", 0, 1)],
]


def make_schedule(batches):
    last = 2 * (batches - 1) + UNIT_GAP

    def exists(u):
        return 0 <= u <= last and u not in (1, last - 1)

    def count(u):
        return sum(exists(v) for v in range(max(u, -1) + 1))

    class Unit:

        def __init__(self, u, j=None):
            self.u, self.j = u, j
            self.layer = u % 2
            self.batch0 = (u - UNIT_GAP * self.layer) // 2
            self.par = u % 2
            self.slot = self.batch0 % 2

        def at(self, d):
            return Unit(self.u + d, self.j)

        @property
        def first(self):
            return self.j is None and self.batch0 == 0

        @property
        def real(self):
            return self.j is not None or exists(self.u)

        def n(self, d=0, m=1, add=0):
            if self.j is None:
                return m * count(self.u + d) + add
            return self.j * (LOOP_SLOTS * m) + (m * (self.u + d) + add)

        def past(self, d):
            return self.j is not None or count(self.u + d) > 0

        def pair0(self):
            n = self.u if self.j is not None else count(self.u)
            return (n - 1) % 2

        def batch(self, m=1, add=0):
            b = m * self.batch0 + add
            return b if self.j is None else self.j * (2 * m) + b

        def turns(self, m=1, add=0):
            b = m * (self.batch0 // 2 + 1) + add
            return b if self.j is None else self.j * m + b

    first, end = 0, last + 4
    lo = 2
    hi = (last - 3) // LOOP_SLOTS
    while LOOP_SLOTS * hi > last - 3:
        hi -= 1

    fills = [(0,) + f for f in START_FILLS]
    for k in range(first, end):
        for kind, part, d in SLOT_FILLS[k % 2]:
            u = k + d
            if u > 0 and exists(u) and not (kind == "C" and u % 2):
                fills.append((u, kind, part))
    order = {f: n for n, f in enumerate(fills)}

    def fill(u, kind, part):
        shift = 0 if u.j is None else LOOP_SLOTS * lo
        n = order[(u.u + shift, kind, part)]
        if n < 2:
            return n % 2, None
        pu, pkind, ppart = fills[n - 2]
        return n % 2, (Unit(pu - shift, u.j), pkind, ppart)

    return Unit, exists, fill, (first, lo, hi, end, last)


def build_xattn(nc, x, ctx, weights, out):
    B, T, E = x.shape
    _, M, L = ctx.shape
    P = 128
    TP, TH = T // 2, 2
    MC = 6
    MP = M // MC
    EC, LC = E // P, L // P
    HALF = MC // 2
    SCALE = float(E) ** -0.5
    assert TP <= P and MP <= P and MP * MC == M and TH * TP == T
    Unit, exists, fill, (FIRST, LO, HI, END, LAST) = make_schedule(B)

    with ExitStack() as stack:
        def sb(name, shape, dt=F32):
            return stack.enter_context(nc.sbuf_tensor(name, shape, dt))

        def bank(name):
            return stack.enter_context(nc.psum_tensor(name, [P, 512], F32))

        def sem(name):
            return stack.enter_context(nc.semaphore(name))

        A_hi = sb("A_hi", [P, LAYERS, EC, L], F32R)
        A_lo = sb("A_lo", [P, LAYERS, EC, L], F32R)
        Wv_hi = sb("Wv_hi", [P, LAYERS, LC, E], F32R)
        Wv_lo = sb("Wv_lo", [P, LAYERS, LC, E], F32R)
        c_col = sb("c_col", [P, LAYERS, LC + 1])
        w_col = sb("w_col", [P, EC])
        w_row = sb("w_row", [P, LAYERS, E])
        bv_row = sb("bv_row", [P, LAYERS, E])
        gamma_row = sb("gamma_row", [P, LAYERS, E])
        beta_row = sb("beta_row", [P, LAYERS, E])
        bq_col = sb("bq_col", [P, LAYERS, EC])
        bk_col = sb("bk_col", [P, LAYERS, EC])
        beta_col = sb("beta_col", [P, EC])
        ident = sb("ident", [P, P])
        ones = sb("ones", [P, 2])
        minus_half = sb("minus_half", [P, 1])

        x0 = sb("x0", [P, 2, TH, E])
        x1 = sb("x1", [P, 2, TH, E])
        y_out = sb("y_out", [P, 2, TH, E])
        raw = sb("raw", [P, 2, MC, L])
        cn_hi = sb("cn_hi", [P, 2, MC, L], F32R)
        cn_lo = sb("cn_lo", [P, 2, MC, L], F32R)
        cT_hi = sb("cT_hi", [P, 2, LC, M], F32R)
        cT_lo = sb("cT_lo", [P, 2, LC, M], F32R)

        xT_hi = sb("xT_hi", [P, EC, T], F32R)
        xT_lo = sb("xT_lo", [P, EC, T], F32R)
        qT_hi = sb("qT_hi", [P, LC, T], F32R)
        qT_lo = sb("qT_lo", [P, LC, T], F32R)
        d_col = sb("d_col", [P, TH])
        d_row = sb("d_row", [P, T])
        dot_junk = sb("dot_junk", [P, E])
        scores = sb("scores", [P, MC, T])
        smax = sb("smax", [P, MC])
        neg_max = sb("neg_max", [P, MC])
        ssum = sb("ssum", [P, MC])
        rsum = sb("rsum", [P, 2, MC])
        probs = sb("probs", [P, 2, MC, T])
        pr_hi = sb("pr_hi", [P, 2, MC, T], F32R)
        pr_lo = sb("pr_lo", [P, 2, MC, T], F32R)
        psum3 = sb("psum3", [P, HALF, T])
        psum1 = sb("psum1", [P, T])
        psum_all = sb("psum_all", [P, T])
        oT_hi = sb("oT_hi", [P, LC, T], F32R)
        oT_lo = sb("oT_lo", [P, LC, T], F32R)
        y = sb("y", [P, 2, TH, E])
        z = sb("z", [P, LAYERS, TH, E])
        bn = sb("bn", [P, 2, TH, 6])
        mv = sb("mv", [P, 2, TH, 2])
        ve = sb("ve", [P, 2, TH])
        rstd = sb("rstd", [P, 2, TH])
        nmr = sb("nmr", [P, 2, TH])

        Wq_raw = y[:, :, :, :].rearrange("p a h e -> p (a h) e")
        WqT = y_out[:, :, :, :].rearrange("p a h e -> p (a h) e")
        Wk_raw = x1[:, 0, :, :]
        Wv_raw = x1[:, 1, :, :]
        WkT = probs[:, 1, :, :].rearrange("p c t -> p (c t)")[:, 0:EC * (L + 1)].rearrange("p (f l) -> p f l", f=EC)

        score_bank = [bank("score_bank0"), bank("score_bank1")]
        t_bank = [bank("t_bank0"), bank("t_bank1")]
        oq_bank = [bank("oq_bank0"), bank("oq_bank1")]
        pv_bank = [bank("pv_bank0"), bank("pv_bank1")]

        r_psum = oq_bank[R_HALF][0:TP, T:T + TH]

        consts_ready = sem("consts_ready")
        q_loaded = [[sem("q_loaded00"), sem("q_loaded01")], [sem("q_loaded10"), sem("q_loaded11")]]
        k_loaded = [sem("k_loaded0"), sem("k_loaded1")]
        v_loaded = [sem("v_loaded0"), sem("v_loaded1")]
        b_loaded = [sem("b_loaded0"), sem("b_loaded1")]
        rows_loaded = [sem("rows_loaded0"), sem("rows_loaded1")]
        wT_ready = sem("wT_ready")
        WqT_done = sem("WqT_done")
        WkT_done = sem("WkT_done")
        beta_ready = sem("beta_ready")
        bq_done = sem("bq_done")
        A_ready = sem("A_ready")
        A_hi_done = sem("A_hi_done")
        A_lo_done = sem("A_lo_done")
        w_ready = sem("w_ready")
        w_done = sem("w_done")
        c_ready = sem("c_ready")
        c_done = sem("c_done")
        Wv_hi_done = sem("Wv_hi_done")
        Wv_lo_done = sem("Wv_lo_done")

        x_loaded = [sem("x_loaded0"), sem("x_loaded1")]
        ctx_loaded = [sem("ctx_loaded0"), sem("ctx_loaded1")]
        stored = [sem("stored0"), sem("stored1")]
        last_stored = sem("last_stored")
        ctxT_ready = sem("ctxT_ready")
        ctxT_hi_done = sem("ctxT_hi_done")
        ctxT_lo_done = sem("ctxT_lo_done")
        cn_hi_done = sem("cn_hi_done")
        cn_done = sem("cn_done")
        xT_ready = sem("xT_ready")
        xT_hi_done = sem("xT_hi_done")
        xT_lo_done = sem("xT_lo_done")
        dot_done = sem("dot_done")
        d_ready = sem("d_ready")
        d_done = sem("d_done")
        q_ready = sem("q_ready")
        qT_hi_done = sem("qT_hi_done")
        qT_lo_done = sem("qT_lo_done")
        s_ready = sem("s_ready")
        smax_done = sem("smax_done")
        neg_max_done = sem("neg_max_done")
        exp_done = sem("exp_done")
        rsum_done = sem("rsum_done")
        probs_done = sem("probs_done")
        pr_hi_done = sem("pr_hi_done")
        pr_lo_done = sem("pr_lo_done")
        psum3_done = sem("psum3_done")
        psum1_done = sem("psum1_done")
        psum_done = sem("psum_done")
        o_ready = sem("o_ready")
        oT_hi_done = sem("oT_hi_done")
        oT_lo_done = sem("oT_lo_done")
        resid_done = sem("resid_done")
        pv_ready = sem("pv_ready")
        y_done = sem("y_done")
        bn_done = sem("bn_done")
        mv_done = sem("mv_done")
        ve_done = sem("ve_done")
        rstd_done = sem("rstd_done")
        nmr_done = sem("nmr_done")
        z_done = sem("z_done")
        zg_done = sem("zg_done")
        ln_done = sem("ln_done")
        last_zg_done = sem("last_zg_done")
        last_ln_done = sem("last_ln_done")

        wait_alone = sem("wait_alone")

        block = stack.enter_context(nc.Block())

        def slots(eng, slot):
            for k in range(FIRST, LOOP_SLOTS * LO):
                slot(k, None)
            with eng.Fori(LO, HI) as j:
                for s in range(LOOP_SLOTS):
                    slot(s, j)
            for k in range(LOOP_SLOTS * HI, END):
                slot(k, None)

        def x_in(u, h):
            return z[0:TP, 0, h, :] if u.layer else x0[0:TP, u.slot, h, :]

        fold_bank = [score_bank + pv_bank, pv_bank]

        @block.sync
        def _(sp):
            def load_qk(l):
                W = weights[l]
                Wq = W["Wq"].rearrange("(c p) f -> p c f", p=P)
                for half in range(2):
                    cols = slice(half * E // 2, (half + 1) * E // 2)
                    sp.dma_start(Wq_raw[:, :, cols], Wq[:, :, cols]).then_inc(q_loaded[l][half], 16)
                sp.dma_start(Wk_raw, W["Wk"].rearrange("(c p) f -> p c f", p=P)).then_inc(k_loaded[l], 16)

            def load_v(l):
                sp.dma_start(Wv_raw, weights[l]["Wv"].rearrange("(c p) e -> p c e", p=P)).then_inc(v_loaded[l], 16)

            def load_rows(l):
                W = weights[l]
                sp.dma_start(bv_row[:, l, :], W["bv"].partition_broadcast(P)).then_inc(rows_loaded[l], 16)
                sp.dma_start(gamma_row[:, l, :], W["gamma"].partition_broadcast(P)).then_inc(rows_loaded[l], 16)
                sp.dma_start(beta_row[:, l, :], W["beta"].partition_broadcast(P)).then_inc(rows_loaded[l], 16)

            def load_x(i):
                sp.dma_start(x0[0:TP, i], x[i].rearrange("(p h) e -> p h e", h=TH)).then_inc(x_loaded[i], 16)

            def load_ctx(i):
                sp.dma_start(raw[0:MP, i], ctx[i].rearrange("(p c) l -> p c l", c=MC)).then_inc(ctx_loaded[i], 16)

            load_qk(0)
            load_x(0)
            load_ctx(0)
            load_rows(0)
            load_v(0)
            sp.wait_ge(wT_ready, 6)
            load_qk(1)
            load_ctx(1)
            load_x(1)
            sp.wait_ge(Wv_lo_done, 1)
            load_v(1)
            load_rows(1)

            def slot(k, j):
                if k % 2 == 0:
                    return
                done, nxt = Unit(k - 2, j), Unit(k + 3, j)
                if j is None and done.u == LAST:
                    rows = out[done.batch()].rearrange("(p h) e -> p h e", h=TH)
                    sp.wait_ge(ln_done, done.n(m=2, add=-1))
                    sp.dma_start(rows[:, 0, :], y_out[0:TP, done.slot, 0, :]).then_inc(stored[done.slot], 16)
                    sp.wait_ge(last_ln_done, 1)
                    sp.dma_start(rows[:, 1, :], y_out[0:TP, done.slot, 1, :]).then_inc(last_stored, 16)
                elif done.real:
                    sp.wait_ge(ln_done, done.n(m=2))
                    sp.sem_inc(wait_alone, 1)
                    sp.dma_start(out[done.batch()].rearrange("(p h) e -> p h e", h=TH),
                                 y_out[0:TP, done.slot]).then_inc(stored[done.slot], 16)
                if nxt.real and k >= 1:
                    sp.wait_ge(resid_done, nxt.n(-4, 2))
                    sp.sem_inc(wait_alone, 1)
                    sp.dma_start(x0[0:TP, nxt.slot],
                                 x[nxt.batch()].rearrange("(p h) e -> p h e", h=TH)).then_inc(x_loaded[nxt.slot], 16)
                    sp.wait_ge(cn_done, nxt.batch(2, -2))
                    sp.sem_inc(wait_alone, 1)
                    sp.dma_start(raw[0:MP, nxt.slot],
                                 ctx[nxt.batch()].rearrange("(p c) l -> p c l", c=MC)).then_inc(ctx_loaded[nxt.slot], 16)

            slots(sp, slot)
            for i in range(2):
                sp.wait_ge(stored[i], 16 * (B // 2))
            sp.wait_ge(last_stored, 16)

        @block.tensor
        def _(pe):
            def transpose_weights(l):
                banks = fold_bank[l]
                for part in range(6):
                    if part in (0, EC // 2):
                        pe.wait_ge(q_loaded[l][part // (EC // 2)], 16)
                    elif part == EC:
                        pe.wait_ge(k_loaded[l], 16)
                    if part >= len(banks):
                        pe.wait_ge(WqT_done, EC * l + part - len(banks) + 1)
                    b = banks[part % len(banks)]
                    if part < EC:
                        for e in range(EC):
                            ins = nc.tensor.transpose(b[:, e * P:(e + 1) * P], Wq_raw[:, e, part * P:(part + 1) * P], ident[:, :])
                    else:
                        for f in range(2):
                            for c in range(LC):
                                at = f * L + c * P
                                ff = 2 * (part - EC) + f
                                ins = nc.tensor.transpose(b[:, at:at + P], Wk_raw[:, c, ff * P:(ff + 1) * P], ident[:, :])
                    ins.then_inc(wT_ready, 1)

            def fold_weights(l):
                banks = fold_bank[l]
                pe.wait_ge(WqT_done, EC * (l + 1))
                pe.wait_ge(WkT_done, 3 * (l + 1))
                if l > 0:
                    pe.wait_ge(bq_done, l)
                for e in range(EC):
                    b = banks[e % len(banks)]
                    if e >= len(banks):
                        pe.wait_ge(A_lo_done, EC * l + e - len(banks) + 1)
                    for f in range(EC):
                        ins = nc.tensor.matmul(b[:, 0:L + 1], WqT[:, f, e * P:(e + 1) * P], WkT[:, f, :],
                                               start=(f == 0), stop=(f == EC - 1))
                    ins.then_inc(A_ready, 1)

            def fold_beta():
                b = fold_bank[1][0]
                pe.wait_ge(WkT_done, 3 + 2)
                pe.wait_ge(b_loaded[1], 16 * 3)
                for f in range(EC):
                    for e in range(EC):
                        ins = nc.tensor.matmul(b[:, f:f + 1], Wq_raw[:, e, f * P:(f + 1) * P], beta_col[:, e:e + 1],
                                               start=(e == 0), stop=(e == EC - 1))
                ins.then_inc(beta_ready, 1)

            def fold_c(l):
                banks = fold_bank[l]
                pe.wait_ge(b_loaded[l], 16 * (2 + l))
                pe.wait_ge(A_lo_done, EC * l + EC - 1)
                b = banks[0]
                for c in range(LC):
                    for f in range(EC):
                        nc.tensor.matmul(b[:, c:c + 1], WkT[:, f, c * P:(c + 1) * P], bq_col[:, l, f:f + 1],
                                         start=(f == 0), stop=(f == EC - 1))
                for f in range(EC):
                    ins = nc.tensor.matmul(b[:, LC:LC + 1], bk_col[:, l, f:f + 1].to_broadcast([P, P]), bq_col[:, l, f:f + 1],
                                           start=(f == 0), stop=(f == EC - 1))
                ins.then_inc(c_ready, 1)

            def fold_w(l):
                pe.wait_ge(A_lo_done, EC * (l + 1))
                b = fold_bank[l][1]
                for e in range(EC):
                    ins = nc.tensor.transpose(b[:, e * P:(e + 1) * P], w_col[:, e:e + 1].to_broadcast([P, P]), ident[:, :])
                ins.then_inc(w_ready, 1)

            def bank_free(u, kind, part):
                b, before = fill(u, kind, part)
                if before:
                    pu, pkind, ppart = before
                    if pkind == "X":
                        pe.wait_ge(xT_lo_done, pu.n(m=2, add=ppart - 1))
                    elif pkind == "C":
                        pe.wait_ge(ctxT_lo_done, pu.batch(3, ppart + 1))
                    else:
                        pe.wait_ge(d_done, pu.n())
                return t_bank[b]

            def transpose_ctx(u, g):
                if u.layer or not u.real:
                    return
                if g == 0:
                    pe.wait_ge(ctx_loaded[u.slot], u.turns(16))
                b = bank_free(u, "C", g)
                for l in range(LC):
                    for c in range(2):
                        at = (l * 2 + c) * MP
                        ins = nc.tensor.transpose(b[:, at:at + MP], raw[0:MP, u.slot, 2 * g + c, l * P:(l + 1) * P],
                                                  ident[0:MP, 0:MP])
                ins.then_inc(ctxT_ready, 1)

            def transpose_x(u, g):
                if not u.real:
                    return
                if g == 0:
                    if u.layer == 0:
                        pe.wait_ge(x_loaded[u.slot], u.turns(16))
                    else:
                        pe.wait_ge(z_done, u.n(-UNIT_GAP, 2))
                b = bank_free(u, "X", g)
                for e in range(2):
                    for h in range(TH):
                        at = e * T + h * TP
                        ee = 2 * g + e
                        ins = nc.tensor.transpose(b[:, at:at + TP], x_in(u, h)[:, ee * P:(ee + 1) * P],
                                                  ident[0:TP, 0:TP])
                ins.then_inc(xT_ready, 1)

            def spread_d(u):
                if not u.real:
                    return
                pe.wait_ge(dot_done, u.n(m=2))
                b = bank_free(u, "D", 0)
                for h in range(TH):
                    ins = nc.tensor.transpose(b[:, h * TP:(h + 1) * TP], d_col[0:TP, h:h + 1].to_broadcast([TP, P]),
                                              ident[0:TP, 0:TP])
                ins.then_inc(d_ready, 1)

            def q_product(u, l):
                if not u.real:
                    return
                if u.first and l == 0:
                    pe.wait_ge(A_lo_done, EC * (u.layer + 1))
                if u.past(-2):
                    pe.wait_ge(oT_lo_done, u.n(-2, 2, l - 1))
                    if l == R_HALF:
                        pe.wait_ge(resid_done, u.n(-2, 2))
                for e in range(EC):
                    if l == 0 and e % 2 == 0:
                        pe.wait_ge(xT_hi_done, u.n(m=2, add=e // 2 - 1))
                        pe.wait_ge(xT_lo_done, u.n(m=2, add=e // 2 - 1))
                    hi = A_hi[:, u.layer, e, l * P:(l + 1) * P]
                    lo = A_lo[:, u.layer, e, l * P:(l + 1) * P]
                    o = oq_bank[l][:, 0:T]
                    nc.tensor.matmul(o, hi, xT_hi[:, e, :], start=(e == 0), stop=False)
                    nc.tensor.matmul(o, hi, xT_lo[:, e, :], start=False, stop=False)
                    ins = nc.tensor.matmul(o, lo, xT_hi[:, e, :], start=False, stop=(e == EC - 1))
                ins.then_inc(q_ready, 1)

            def score_product(u, p):
                if not u.real:
                    return
                if u.layer == 0:
                    pe.wait_ge(ctxT_hi_done, u.batch(3, p + 1))
                    pe.wait_ge(ctxT_lo_done, u.batch(3, p + 1))
                if u.past(-1) or p == 2:
                    pe.wait_ge(smax_done, u.n(m=6, add=2 * p - 8))
                b = score_bank[(u.pair0() + p) % 2]
                for c in range(2):
                    cols = slice((2 * p + c) * MP, (2 * p + c + 1) * MP)
                    o = b[0:MP, c * T:(c + 1) * T]
                    for l in range(LC):
                        if p == 0 and c == 0:
                            pe.wait_ge(qT_hi_done, u.n(m=2, add=l - 1))
                            pe.wait_ge(qT_lo_done, u.n(m=2, add=l - 1))
                        hi, lo = cT_hi[:, u.slot, l, cols], cT_lo[:, u.slot, l, cols]
                        nc.tensor.matmul(o, hi, qT_hi[:, l, :], start=(l == 0), stop=False)
                        nc.tensor.matmul(o, hi, qT_lo[:, l, :], start=False, stop=False)
                        ins = nc.tensor.matmul(o, lo, qT_hi[:, l, :], start=False, stop=(l == LC - 1))
                ins.then_inc(s_ready, 1)

            def o_product(u, l):
                if not u.real:
                    return
                if u.layer == 0:
                    pe.wait_ge(cn_done, u.batch(2, l + 1))
                o = oq_bank[l][:, 0:T]
                for c in range(MC):
                    if l == 0 and c % HALF == 0:
                        pe.wait_ge(pr_hi_done, u.n(m=2, add=c // HALF - 1))
                        pe.wait_ge(pr_lo_done, u.n(m=2, add=c // HALF - 1))
                    hi = cn_hi[0:MP, u.slot, c, l * P:(l + 1) * P]
                    lo = cn_lo[0:MP, u.slot, c, l * P:(l + 1) * P]
                    nc.tensor.matmul(o, hi, pr_hi[0:MP, u.par, c, :], start=(c == 0), stop=False)
                    nc.tensor.matmul(o, hi, pr_lo[0:MP, u.par, c, :], start=False, stop=False)
                    ins = nc.tensor.matmul(o, lo, pr_hi[0:MP, u.par, c, :], start=False, stop=(c == MC - 1))
                if l == R_HALF:
                    pe.wait_ge(psum_done, u.n())
                    for h in range(TH):
                        ins = nc.tensor.matmul(r_psum[:, h:h + 1], psum_all[0:MP, h * TP:(h + 1) * TP], ones[0:MP, 0:1],
                                               start=True, stop=True)
                ins.then_inc(o_ready, 1)

            def pv_product(u, h):
                if not u.real:
                    return
                if u.past(-1):
                    pe.wait_ge(y_done, u.n(-1, 2, h - 1))
                if u.first and h == 0:
                    pe.wait_ge(Wv_lo_done, u.layer + 1)
                    pe.wait_ge(c_done, u.layer + 1)
                    pe.wait_ge(w_done, u.layer + 1)
                o = pv_bank[h][0:TP, :]
                for l in range(LC):
                    if h == 0:
                        pe.wait_ge(oT_hi_done, u.n(m=2, add=l - 1))
                        pe.wait_ge(oT_lo_done, u.n(m=2, add=l - 1))
                    rows = slice(h * TP, (h + 1) * TP)
                    hi, lo = oT_hi[:, l, rows], oT_lo[:, l, rows]
                    nc.tensor.matmul(o, hi, Wv_hi[:, u.layer, l, :], start=(l == 0), stop=False)
                    nc.tensor.matmul(o, hi, Wv_lo[:, u.layer, l, :], start=False, stop=False)
                    ins = nc.tensor.matmul(o, lo, Wv_hi[:, u.layer, l, :], start=False, stop=(l == LC - 1))
                ins.then_inc(pv_ready, 1)

            u0 = Unit(0)
            pe.wait_ge(consts_ready, 4)
            transpose_weights(0)
            transpose_x(u0, 0)
            transpose_x(u0, 1)
            fold_weights(0)
            fold_c(0)
            fold_w(0)
            transpose_ctx(u0, 0)
            transpose_ctx(u0, 1)
            q_product(u0, 0)
            q_product(u0, 1)
            transpose_ctx(u0, 2)
            spread_d(u0)
            pe.wait_ge(c_done, 1)
            pe.wait_ge(w_done, 1)

            def slot(k, j):
                nxt, now, last = Unit(k + 1, j), Unit(k, j), Unit(k - 1, j)
                if k % 2 == 0:
                    if now.u > 0 or j is not None:
                        transpose_ctx(now, 2)
                    score_product(now, 0)
                    score_product(now, 1)
                    o_product(last, 0)
                    score_product(now, 2)
                    if j is None and k == 0:
                        transpose_weights(1)
                        fold_beta()
                        fold_weights(1)
                    if j is None and k == 2:
                        fold_c(1)
                        fold_w(1)
                    o_product(last, 1)
                    transpose_x(nxt, 0)
                    transpose_x(nxt, 1)
                    pv_product(last, 0)
                    pv_product(last, 1)
                    q_product(nxt, 0)
                    q_product(nxt, 1)
                else:
                    spread_d(now)
                    transpose_ctx(nxt, 0)
                    score_product(now, 0)
                    transpose_ctx(nxt, 1)
                    score_product(now, 1)
                    score_product(now, 2)
                    o_product(last, 0)
                    o_product(last, 1)
                    transpose_x(nxt, 0)
                    transpose_x(nxt, 1)
                    pv_product(last, 0)
                    q_product(nxt, 0)
                    q_product(nxt, 1)
                    pv_product(last, 1)
                    spread_d(nxt)

            slots(pe, slot)

        @block.scalar
        def _(act):
            for l in range(LAYERS):
                W = weights[l]
                act.dma_start(bq_col[:, l, :], W["bq"].rearrange("(c p) -> p c", p=P),
                              allow_slow_non_contiguous=True).then_inc(b_loaded[l], 16)
                act.dma_start(bk_col[:, l, :], W["bk"].rearrange("(c p) -> p c", p=P),
                              allow_slow_non_contiguous=True).then_inc(b_loaded[l], 16)
            act.dma_start(beta_col[:, :], weights[0]["beta"].rearrange("(c p) -> p c", p=P),
                          allow_slow_non_contiguous=True).then_inc(b_loaded[1], 16)

            def WkT_out(l):
                if l:
                    act.wait_ge(c_ready, l)
                act.wait_ge(b_loaded[l], 16 * (2 + l))
                act.activation(WkT[:, :, L:L + 1], bk_col[:, l, :].unsqueeze(2), ACT.Identity).then_inc(WkT_done, 1)
                for g in range(2):
                    b = fold_bank[l][(EC + g) % len(fold_bank[l])]
                    act.wait_ge(wT_ready, 6 * l + EC + g + 1)
                    act.activation(WkT[:, 2 * g:2 * g + 2, 0:L], b[:, :].rearrange("p (f l) -> p f l", f=2),
                                   ACT.Identity).then_inc(WkT_done, 1)

            def A_hi_part(l):
                for e in range(EC):
                    act.wait_ge(A_ready, EC * l + e + 1)
                    act.activation(A_hi[:, l, e, :], fold_bank[l][e % len(fold_bank[l])][:, 0:L], ACT.Identity).then_inc(A_hi_done, 1)

            def Wv_hi_part(l):
                act.wait_ge(v_loaded[l], 16)
                act.activation(Wv_hi[:, l, :, :], Wv_raw, ACT.Identity).then_inc(Wv_hi_done, 1)

            def ctxT_hi(u, g):
                if u.layer or not u.real:
                    return
                act.wait_ge(ctxT_ready, u.batch(3, g + 1))
                b = t_bank[fill(u, "C", g)[0]]
                act.activation(cT_hi[:, u.slot, :, 2 * g * MP:(2 * g + 2) * MP],
                               b[:, 0:4 * MP].rearrange("p (l m) -> p l m", l=LC), ACT.Identity).then_inc(ctxT_hi_done, 1)

            def ctx_hi(u, l):
                if u.layer or not u.real:
                    return
                cols = slice(l * P, (l + 1) * P)
                if l == 0:
                    act.wait_ge(ctx_loaded[u.slot], u.turns(16))
                if u.past(-1):
                    act.wait_ge(o_ready, u.n(-1, 2, l - 1))
                act.activation(cn_hi[0:MP, u.slot, :, cols], raw[0:MP, u.slot, :, cols], ACT.Identity).then_inc(cn_hi_done, 1)

            def xT_hi_part(u, g):
                if not u.real:
                    return
                act.wait_ge(xT_ready, u.n(m=2, add=g - 1))
                if u.past(-1) and g == 0:
                    act.wait_ge(q_ready, u.n(-1, 2))
                b = t_bank[fill(u, "X", g)[0]]
                act.activation(xT_hi[:, 2 * g:2 * g + 2, :], b[:, 0:2 * T].rearrange("p (e t) -> p e t", e=2),
                               ACT.Identity).then_inc(xT_hi_done, 1)

            def d_out(u):
                if not u.real:
                    return
                act.wait_ge(d_ready, u.n())
                if u.past(-1):
                    act.wait_ge(smax_done, u.n(-1, 6))
                act.activation(d_row[:, :], t_bank[fill(u, "D", 0)[0]][:, 0:T], ACT.Identity).then_inc(d_done, 1)

            def q_hi(u, l):
                if not u.real:
                    return
                act.wait_ge(q_ready, u.n(m=2, add=l - 1))
                if u.past(-1) and l == 0:
                    act.wait_ge(s_ready, u.n(-1, 3))
                if u.first and l == 0:
                    act.wait_ge(c_done, u.layer + 1)
                act.activation(qT_hi[:, l, :], oq_bank[l][:, 0:T], ACT.Identity,
                               bias=c_col[:, u.layer, l:l + 1]).then_inc(qT_hi_done, 1)

            def exps(u, half):
                if not u.real:
                    return
                act.wait_ge(neg_max_done, u.n(m=2, add=half - 1))
                if u.past(-2) and half == 0:
                    act.wait_ge(pr_lo_done, u.n(-2, 2))
                    act.wait_ge(psum3_done, u.n(-2))
                for c in range(HALF * half, HALF * (half + 1)):
                    ins = act.activation(probs[0:MP, u.par, c, :], scores[0:MP, c, :], ACT.Exp,
                                         bias=neg_max[0:MP, c:c + 1], scale=SCALE, accum_out=ssum[0:MP, c:c + 1])
                ins.then_inc(exp_done, 1)

            def normalise(u, half):
                if not u.real:
                    return
                act.wait_ge(rsum_done, u.n(m=2, add=half - 1))
                for c in range(HALF * half, HALF * (half + 1)):
                    ins = act.activation(probs[0:MP, u.par, c, :], probs[0:MP, u.par, c, :], ACT.Identity,
                                         scale=rsum[0:MP, u.par, c:c + 1])
                ins.then_inc(probs_done, 1)

            def probs_hi(u, half):
                if not u.real:
                    return
                chunks = slice(HALF * half, HALF * (half + 1))
                act.wait_ge(probs_done, u.n(m=2, add=half - 1))
                if u.past(-2) and half == 0:
                    act.wait_ge(o_ready, u.n(-2, 2))
                act.activation(pr_hi[0:MP, u.par, chunks, :], probs[0:MP, u.par, chunks, :], ACT.Identity).then_inc(pr_hi_done, 1)

            def o_hi(u, l):
                if not u.real:
                    return
                act.wait_ge(o_ready, u.n(m=2, add=l - 1))
                if u.past(-1) and l == 0:
                    act.wait_ge(pv_ready, u.n(-1, 2))
                act.activation(oT_hi[:, l, :], oq_bank[l][:, 0:T], ACT.Identity).then_inc(oT_hi_done, 1)

            def standardise(u, h):
                if not u.real:
                    return
                act.wait_ge(nmr_done, u.n(m=2, add=h - 1))
                if u.past(-2):
                    act.wait_ge(zg_done, u.n(-2, 2, h - 1))
                    if u.layer == 0:
                        act.wait_ge(xT_ready, u.n(1, 2))
                        act.wait_ge(dot_done, u.n(1, 2))
                act.activation(z[0:TP, u.layer, h, :], y[0:TP, u.par, h, :], ACT.Identity, bias=nmr[0:TP, u.par, h:h + 1],
                               scale=rstd[0:TP, u.par, h:h + 1]).then_inc(z_done, 1)

            u0 = Unit(0)
            WkT_out(0)
            xT_hi_part(u0, 0)
            xT_hi_part(u0, 1)
            A_hi_part(0)
            ctxT_hi(u0, 0)
            ctxT_hi(u0, 1)
            q_hi(u0, 0)
            q_hi(u0, 1)
            ctxT_hi(u0, 2)
            Wv_hi_part(0)
            d_out(u0)

            def slot(k, j):
                nxt, now, last, prev = Unit(k + 1, j), Unit(k, j), Unit(k - 1, j), Unit(k - 2, j)
                if k % 2 == 0:
                    exps(now, 0)
                    exps(now, 1)
                    if j is None and k == 0:
                        WkT_out(1)
                    if j is None and k == 2:
                        Wv_hi_part(1)
                    o_hi(last, 1)
                    xT_hi_part(nxt, 0)
                    ctx_hi(now, 0)
                    xT_hi_part(nxt, 1)
                    normalise(now, 0)
                    probs_hi(now, 0)
                    normalise(now, 1)
                    q_hi(nxt, 0)
                    q_hi(nxt, 1)
                    ctx_hi(now, 1)
                    d_out(nxt)
                    probs_hi(now, 1)
                    if j is None and k == 0:
                        A_hi_part(1)
                    standardise(last, 0)
                    exps(nxt, 0)
                else:
                    ctxT_hi(nxt, 0)
                    o_hi(last, 0)
                    ctxT_hi(nxt, 1)
                    exps(now, 1)
                    o_hi(last, 1)
                    xT_hi_part(nxt, 0)
                    xT_hi_part(nxt, 1)
                    normalise(now, 0)
                    standardise(prev, 1)
                    probs_hi(now, 0)
                    q_hi(nxt, 0)
                    q_hi(nxt, 1)
                    normalise(now, 1)
                    d_out(nxt)
                    probs_hi(now, 1)
                    ctxT_hi(nxt, 2)
                    standardise(last, 0)
                    o_hi(now, 0)
                    standardise(last, 1)

            slots(act, slot)

        @block.vector
        def _(dve):
            def WqT_out(l):
                if l:
                    dve.wait_ge(w_ready, l)
                    dve.wait_ge(rows_loaded[0], 16 * 3)
                for part in range(EC):
                    dve.wait_ge(wT_ready, 6 * l + part + 1)
                    b = fold_bank[l][part % len(fold_bank[l])]
                    if l:
                        dve.tensor_tensor(WqT[:, part, :], b[:, :], gamma_row[:, 0, :], ALU.mult).then_inc(WqT_done, 1)
                    else:
                        dve.tensor_copy(WqT[:, part, :], b[:, :]).then_inc(WqT_done, 1)

            def add_beta_to_bq():
                dve.wait_ge(beta_ready, 1)
                dve.wait_ge(b_loaded[1], 16 * 3)
                dve.tensor_tensor(bq_col[:, 1, :], fold_bank[1][0][:, 0:EC], bq_col[:, 1, :], ALU.add).then_inc(bq_done, 1)

            def A_lo_part(l):
                if l:
                    dve.wait_ge(w_ready, l)
                for e in range(EC):
                    b = fold_bank[l][e % len(fold_bank[l])]
                    dve.wait_ge(A_hi_done, EC * l + e + 1)
                    dve.tensor_tensor(A_lo[:, l, e, :], b[:, 0:L], A_hi[:, l, e, :].bitcast(F32), ALU.subtract)
                    dve.tensor_copy(w_col[:, e:e + 1], b[:, L:L + 1]).then_inc(A_lo_done, 1)

            def take_c(l):
                dve.wait_ge(c_ready, l + 1)
                dve.tensor_copy(c_col[:, l, :], fold_bank[l][0][:, 0:LC + 1]).then_inc(c_done, 1)

            def take_w(l):
                dve.wait_ge(w_ready, l + 1)
                dve.tensor_copy(w_row[:, l, :], fold_bank[l][1][:, 0:E]).then_inc(w_done, 1)

            def Wv_lo_part(l):
                dve.wait_ge(Wv_hi_done, l + 1)
                dve.tensor_tensor(Wv_lo[:, l, :, :], Wv_raw, Wv_hi[:, l, :, :].bitcast(F32), ALU.subtract).then_inc(Wv_lo_done, 1)

            def ctxT_lo(u, g):
                if u.layer or not u.real:
                    return
                dve.wait_ge(ctxT_hi_done, u.batch(3, g + 1))
                b = t_bank[fill(u, "C", g)[0]]
                cols = slice(2 * g * MP, (2 * g + 2) * MP)
                dve.tensor_tensor(cT_lo[:, u.slot, :, cols], b[:, 0:4 * MP].rearrange("p (l m) -> p l m", l=LC),
                                  cT_hi[:, u.slot, :, cols].bitcast(F32), ALU.subtract).then_inc(ctxT_lo_done, 1)

            def xT_lo_part(u, g):
                if not u.real:
                    return
                dve.wait_ge(xT_hi_done, u.n(m=2, add=g - 1))
                b = t_bank[fill(u, "X", g)[0]]
                dve.tensor_tensor(xT_lo[:, 2 * g:2 * g + 2, :], b[:, 0:2 * T].rearrange("p (e t) -> p e t", e=2),
                                  xT_hi[:, 2 * g:2 * g + 2, :].bitcast(F32), ALU.subtract).then_inc(xT_lo_done, 1)

            def dot(u, h):
                if not u.real:
                    return
                if h == 0:
                    if u.first:
                        dve.wait_ge(w_done, u.layer + 1)
                        dve.wait_ge(c_done, u.layer + 1)
                    if u.layer == 0:
                        dve.wait_ge(x_loaded[u.slot], u.turns(16))
                    else:
                        dve.wait_ge(z_done, u.n(-UNIT_GAP, 2))
                    if u.past(-1):
                        dve.wait_ge(d_ready, u.n(-1))
                if u.past(-1) or h:
                    dve.wait_ge(dot_done, u.n(m=2, add=h - 2))
                dve.tensor_tensor_reduce(dot_junk[0:TP, :], x_in(u, h), w_row[0:TP, u.layer, :], 1.0,
                                         c_col[0:TP, u.layer, LC:LC + 1], ALU.mult, ALU.add,
                                         d_col[0:TP, h:h + 1]).then_inc(dot_done, 1)

            def q_lo(u, l):
                if not u.real:
                    return
                if u.first and l == 0:
                    dve.wait_ge(c_done, u.layer + 1)
                dve.wait_ge(qT_hi_done, u.n(m=2, add=l - 1))
                dve.scalar_tensor_tensor(out=qT_lo[:, l, :], in0=oq_bank[l][:, 0:T],
                                         scalar=c_col[:, u.layer, l:l + 1], in1=qT_hi[:, l, :].bitcast(F32),
                                         op0=ALU.add, op1=ALU.subtract).then_inc(qT_lo_done, 1)

            def score_max(u, c):
                if not u.real:
                    return
                if c == 0:
                    dve.wait_ge(d_done, u.n())
                    if u.past(-1):
                        dve.wait_ge(exp_done, u.n(-1, 2))
                if c % 2 == 0:
                    dve.wait_ge(s_ready, u.n(m=3, add=c // 2 - 2))
                    dve.sem_inc(wait_alone, 1)
                b = score_bank[(u.pair0() + c // 2) % 2]
                dve.tensor_tensor_reduce(scores[0:MP, c, :], b[0:MP, (c % 2) * T:(c % 2 + 1) * T], d_row[0:MP, :], 1.0,
                                         -3.4e38, ALU.add, ALU.max, smax[0:MP, c:c + 1]).then_inc(smax_done, 1)

            def negate_max(u, half):
                if not u.real:
                    return
                cols = slice(HALF * half, HALF * (half + 1))
                dve.wait_ge(smax_done, u.n(m=6, add=HALF * (half + 1) - 6))
                dve.tensor_scalar(neg_max[0:MP, cols], smax[0:MP, cols], -SCALE, None, ALU.mult).then_inc(neg_max_done, 1)

            def invert_sum(u, half):
                if not u.real:
                    return
                cols = slice(HALF * half, HALF * (half + 1))
                dve.wait_ge(exp_done, u.n(m=2, add=half - 1))
                dve.reciprocal(rsum[0:MP, u.par, cols], ssum[0:MP, cols]).then_inc(rsum_done, 1)

            def probs_lo(u, half):
                if not u.real:
                    return
                chunks = slice(HALF * half, HALF * (half + 1))
                dve.wait_ge(pr_hi_done, u.n(m=2, add=half - 1))
                dve.tensor_tensor(pr_lo[0:MP, u.par, chunks, :], probs[0:MP, u.par, chunks, :],
                                  pr_hi[0:MP, u.par, chunks, :].bitcast(F32), ALU.subtract).then_inc(pr_lo_done, 1)

            def o_lo(u, l):
                if not u.real:
                    return
                dve.wait_ge(oT_hi_done, u.n(m=2, add=l - 1))
                dve.tensor_tensor(oT_lo[:, l, :], oq_bank[l][:, 0:T], oT_hi[:, l, :].bitcast(F32),
                                  ALU.subtract).then_inc(oT_lo_done, 1)

            def residual(u, h):
                if not u.real:
                    return
                if h == 0:
                    dve.wait_ge(oT_hi_done, u.n(m=2, add=R_HALF - 1))
                    if u.first:
                        dve.wait_ge(rows_loaded[u.layer], 16 * 3)
                if u.past(-2):
                    dve.wait_ge(z_done, u.n(-2, 2, h - 1))
                if u.layer and h == 0:
                    dve.wait_ge(ln_done, u.n(-UNIT_GAP, 2))
                dve.scalar_tensor_tensor(out=y[0:TP, u.par, h, :], in0=bv_row[0:TP, u.layer, :], scalar=r_psum[:, h:h + 1],
                                         in1=(x0, x1)[u.layer][0:TP, u.slot, h, :],
                                         op0=ALU.mult, op1=ALU.add).then_inc(resid_done, 1)

            def add_pv(u, h):
                if not u.real:
                    return
                dve.wait_ge(pv_ready, u.n(m=2, add=h - 1))
                dve.wait_ge(resid_done, u.n(m=2, add=h - 1))
                dve.tensor_tensor(y[0:TP, u.par, h, :], pv_bank[h][0:TP, :], y[0:TP, u.par, h, :], ALU.add).then_inc(y_done, 1)

            def half_moments(u, h):
                if not u.real:
                    return
                dve.wait_ge(y_done, u.n(m=2, add=h - 1))
                dve.bn_stats(bn[0:TP, u.par, h, :], y[0:TP, u.par, h, :]).then_inc(bn_done, 1)

            def moments(u, h):
                if not u.real:
                    return
                dve.wait_ge(bn_done, u.n(m=2, add=h - 1))
                dve.sem_inc(wait_alone, 1)
                dve.bn_aggr(mv[0:TP, u.par, h, :], bn[0:TP, u.par, h, :]).then_inc(mv_done, 1)

            def add_eps(u, h):
                if not u.real:
                    return
                dve.wait_ge(mv_done, u.n(m=2, add=h - 1))
                dve.tensor_scalar(ve[0:TP, u.par, h:h + 1], mv[0:TP, u.par, h, 1:2], EPS, None, ALU.add).then_inc(ve_done, 1)

            def shift(u, h):
                if not u.real:
                    return
                dve.wait_ge(rstd_done, u.n(m=2, add=h - 1))
                dve.scalar_tensor_tensor(out=nmr[0:TP, u.par, h:h + 1], in0=mv[0:TP, u.par, h, 0:1], scalar=-1.0,
                                         in1=rstd[0:TP, u.par, h:h + 1], op0=ALU.mult, op1=ALU.mult).then_inc(nmr_done, 1)

            def finish(u, h):
                dve.wait_ge(z_done, u.n(m=2, add=h - 1))
                dve.wait_ge(stored[u.slot], u.turns(16, -16))
                o = y_out[0:TP, u.slot, h, :]
                dve.tensor_tensor(o, z[0:TP, u.layer, h, :], gamma_row[0:TP, u.layer, :], ALU.mult).then_inc(last_zg_done, 1)
                dve.wait_ge(last_zg_done, 1)
                dve.tensor_tensor(o, o, beta_row[0:TP, u.layer, :], ALU.add).then_inc(last_ln_done, 1)

            u0 = Unit(0)
            WqT_out(0)
            xT_lo_part(u0, 0)
            xT_lo_part(u0, 1)
            A_lo_part(0)
            take_c(0)
            ctxT_lo(u0, 0)
            ctxT_lo(u0, 1)
            take_w(0)
            dot(u0, 0)
            dot(u0, 1)
            q_lo(u0, 0)
            q_lo(u0, 1)
            ctxT_lo(u0, 2)

            def slot(k, j):
                nxt, now, last, prev = Unit(k + 1, j), Unit(k, j), Unit(k - 1, j), Unit(k - 2, j)
                if k % 2 == 0:
                    shift(prev, 0)
                    probs_lo(last, 1)
                    half_moments(prev, 1)
                    score_max(now, 0)
                    if now.u > 0 or j is not None:
                        ctxT_lo(now, 2)
                    moments(prev, 1)
                    add_eps(prev, 1)
                    score_max(now, 1)
                    score_max(now, 2)
                    score_max(now, 3)
                    negate_max(now, 0)
                    shift(prev, 1)
                    o_lo(last, 0)
                    score_max(now, 4)
                    score_max(now, 5)
                    negate_max(now, 1)
                    if j is None and k == 0:
                        WqT_out(1)
                        add_beta_to_bq()
                    invert_sum(now, 0)
                    o_lo(last, 1)
                    invert_sum(now, 1)
                    if j is None and k == 0:
                        Wv_lo_part(0)
                    if j is None and k == 2:
                        take_c(1)
                        take_w(1)
                        Wv_lo_part(1)
                    residual(last, 0)
                    residual(last, 1)
                    xT_lo_part(nxt, 0)
                    xT_lo_part(nxt, 1)
                    dot(nxt, 0)
                    add_pv(last, 0)
                    dot(nxt, 1)
                    half_moments(last, 0)
                    q_lo(nxt, 0)
                    q_lo(nxt, 1)
                    moments(last, 0)
                    add_eps(last, 0)
                    add_pv(last, 1)
                    probs_lo(now, 0)
                    score_max(nxt, 0)
                    score_max(nxt, 1)
                    shift(last, 0)
                    half_moments(last, 1)
                    probs_lo(now, 1)
                    if j is None and k == 0:
                        A_lo_part(1)
                    score_max(nxt, 2)
                    negate_max(nxt, 0)
                    score_max(nxt, 3)
                    moments(last, 1)
                    score_max(nxt, 4)
                    score_max(nxt, 5)
                else:
                    negate_max(now, 1)
                    add_eps(prev, 1)
                    ctxT_lo(nxt, 0)
                    invert_sum(now, 0)
                    ctxT_lo(nxt, 1)
                    shift(prev, 1)
                    dot(nxt, 0)
                    o_lo(last, 0)
                    invert_sum(now, 1)
                    o_lo(last, 1)
                    residual(last, 0)
                    xT_lo_part(nxt, 0)
                    xT_lo_part(nxt, 1)
                    residual(last, 1)
                    add_pv(last, 0)
                    half_moments(last, 0)
                    dot(nxt, 1)
                    q_lo(nxt, 0)
                    moments(last, 0)
                    q_lo(nxt, 1)
                    add_eps(last, 0)
                    probs_lo(now, 0)
                    add_pv(last, 1)

            slots(dve, slot)
            finish(Unit(LAST), 1)

        @block.gpsimd
        def _(pool):
            pool.memset(ident[:, :], 0.0).then_inc(consts_ready, 1)
            pool.memset(ones[:, :], 1.0).then_inc(consts_ready, 1)
            pool.memset(minus_half[:, :], -0.5).then_inc(consts_ready, 1)
            pool.wait_ge(consts_ready, 3)
            pool.affine_select(out=ident[:, :], in_=ident[:, :], compare_op=ALU.not_equal, fill=1.0, base=0,
                               pattern=[[-1, P]], channel_multiplier=1).then_inc(consts_ready, 1)
            pool.wait_ge(consts_ready, 4)
            for l in range(LAYERS):
                pool.wait_ge(rows_loaded[l], 16 * 3)

            def ctx_lo(u, l):
                if u.layer or not u.real:
                    return
                cols = slice(l * P, (l + 1) * P)
                pool.wait_ge(cn_hi_done, u.batch(2, l + 1))
                pool.tensor_tensor(cn_lo[0:MP, u.slot, :, cols], raw[0:MP, u.slot, :, cols],
                                   cn_hi[0:MP, u.slot, :, cols].bitcast(F32), ALU.subtract).then_inc(cn_done, 1)

            def sum_probs(u):
                if not u.real:
                    return
                pool.wait_ge(probs_done, u.n(m=2))
                pool.tensor_tensor(psum3[0:MP, :, :], probs[0:MP, u.par, 0:HALF, :], probs[0:MP, u.par, HALF:MC, :],
                                   ALU.add).then_inc(psum3_done, 1)
                pool.wait_ge(psum3_done, u.n())
                pool.tensor_tensor(psum1[0:MP, :], psum3[0:MP, 0, :], psum3[0:MP, 1, :], ALU.add).then_inc(psum1_done, 1)
                pool.wait_ge(psum1_done, u.n())
                if u.past(-1):
                    pool.wait_ge(o_ready, u.n(-1, 2, R_HALF - 1))
                pool.tensor_tensor(psum_all[0:MP, :], psum1[0:MP, :], psum3[0:MP, 2, :], ALU.add).then_inc(psum_done, 1)

            def inverse_deviation(u, h):
                if not u.real:
                    return
                pool.wait_ge(ve_done, u.n(m=2, add=h - 1))
                pool.tensor_tensor(rstd[0:TP, u.par, h:h + 1], ve[0:TP, u.par, h:h + 1], minus_half[0:TP, :],
                                   ALU.pow).then_inc(rstd_done, 1)

            def scale(u, h):
                if not u.real:
                    return
                if u.j is None and u.u == LAST and h == 1:
                    return
                pool.wait_ge(z_done, u.n(m=2, add=h - 1))
                if u.layer == 0:
                    if u.past(-1) and h == 0:
                        pool.wait_ge(resid_done, u.n(-1, 2))
                elif (u.j is not None or u.batch0 >= 2) and h == 0:
                    pool.wait_ge(stored[u.slot], u.turns(16, -16))
                pool.tensor_tensor((x1, y_out)[u.layer][0:TP, u.slot, h, :], z[0:TP, u.layer, h, :], gamma_row[0:TP, u.layer, :],
                                   ALU.mult).then_inc(zg_done, 1)

            def add_beta(u, h):
                if not u.real:
                    return
                if u.j is None and u.u == LAST and h == 1:
                    return
                pool.wait_ge(zg_done, u.n(m=2, add=h - 1))
                o = (x1, y_out)[u.layer][0:TP, u.slot, h, :]
                pool.tensor_tensor(o, o, beta_row[0:TP, u.layer, :], ALU.add).then_inc(ln_done, 1)


            def slot(k, j):
                nxt, now, last, prev = Unit(k + 1, j), Unit(k, j), Unit(k - 1, j), Unit(k - 2, j)
                if k % 2 == 0:
                    scale(prev, 0)
                    scale(prev, 1)
                    add_beta(prev, 0)
                    ctx_lo(now, 0)
                    inverse_deviation(last, 0)
                    add_beta(prev, 1)
                    ctx_lo(now, 1)
                    sum_probs(now)
                    inverse_deviation(last, 1)
                    scale(last, 0)
                    add_beta(last, 0)
                    scale(last, 1)
                    add_beta(last, 1)
                    inverse_deviation(now, 0)
                    sum_probs(nxt)
                    inverse_deviation(now, 1)

            slots(pool, slot)


_NAMES = ("Wq", "bq", "Wk", "bk", "Wv", "bv", "gamma", "beta")


def kernel(**inputs):
    import numpy as _np
    import concourse.bacc as _bacc
    from concourse import mybir as _mybir
    from concourse.bass_utils import run_bass_kernel_spmd as _run

    nc = _bacc.Bacc("TRN2", target_bir_lowering=False, num_devices=1)
    arrays = {}

    def given(name):
        a = _np.ascontiguousarray(inputs[name])
        arrays[f"in_{name}_dram"] = a
        return nc.dram_tensor(f"in_{name}_dram", a.shape, _mybir.dt.from_np(a.dtype), kind="ExternalInput").ap()

    x = given("x")
    ctx = given("ctx_512")
    weights = [{n: given(f"L{l}_xattn_{n}") for n in _NAMES} for l in range(LAYERS)]
    out = nc.dram_tensor("out_0_dram", x.shape, _mybir.dt.float32, kind="ExternalOutput").ap()
    build_xattn(nc, x, ctx, weights, out)
    r = _run(nc, [arrays], core_ids=[0])
    return r.results[0]["out_0_dram"]
```
